# Optimizing a Trainium2 kernel written in Bass

```python
import numpy as np
import jax
import jax.numpy as jnp

def _softmax(x, axis=-1):
    return jax.nn.softmax(x, axis=axis)
def _gelu(x):
    return jax.nn.gelu(x, approximate=True)
def _silu(x):
    return jax.nn.silu(x)
def _sigmoid(x):
    return jax.nn.sigmoid(x)
def _layernorm(x, axis=-1, eps=1e-5):
    m = jnp.mean(x, axis=axis, keepdims=True)
    v = jnp.var(x, axis=axis, keepdims=True)
    return (x - m) / jnp.sqrt(v + eps)
def _scatter_add(tgt, idx, src, axis=0):
    return tgt.at[idx].add(src)
def _segment_sum(src, seg, n):
    return jax.ops.segment_sum(src, seg, n)

kernel_name = 'mk_conv_preact_d1_conv_nchw64_8447ec'

def setup_inputs(seed: int = 0):
    np.random.seed(seed)
    _w = jnp.asarray
    def _rec_inputs():
        import jax
        import jax.numpy as jnp
        _gk = jax.random.key(seed)
        x = -0.0009438 + 1 * jax.random.normal(jax.random.fold_in(_gk, 1), (2, 64, 96, 96), jnp.float32)
        return x
    x = _rec_inputs()
    def _L0_conv_setup():
        import jax, jax.numpy as jnp
        import numpy as np
        C = 64

        def conv1x1(x, w, b):
            return jnp.einsum('bchw,oc->bohw', x, w) + b[None, :, None, None]
        key = jax.random.key(seed)
        ks = jax.random.split(key, 7)
        B, H, W = (2, 96, 96)
        s = 1.0 / np.sqrt(C)
        return {'frame': jax.random.normal(ks[0], (B, C, H, W), dtype=jnp.float32), 'theta_w': jax.random.uniform(ks[1], (C, C), jnp.float32, -s, s), 'theta_b': jax.random.uniform(ks[2], (C,), jnp.float32, -s, s), 'phi_w': jax.random.uniform(ks[3], (C, C), jnp.float32, -s, s), 'phi_b': jax.random.uniform(ks[4], (C,), jnp.float32, -s, s), 'W_w': jax.random.uniform(ks[5], (C, C), jnp.float32, -s, s), 'W_b': jax.random.uniform(ks[6], (C,), jnp.float32, -s, s)}
    _L0_conv_all = _L0_conv_setup()
    _L0_conv_in = {k: v for k, v in _L0_conv_all.items() if k in ('theta_w', 'theta_b', 'phi_w', 'phi_b', 'W_w', 'W_b', )}
    del _L0_conv_all

    return {
        "x": x,
        "L0_conv_theta_w": _L0_conv_in["theta_w"],
        "L0_conv_theta_b": _L0_conv_in["theta_b"],
        "L0_conv_phi_w": _L0_conv_in["phi_w"],
        "L0_conv_phi_b": _L0_conv_in["phi_b"],
        "L0_conv_W_w": _L0_conv_in["W_w"],
        "L0_conv_W_b": _L0_conv_in["W_b"],
    }

def reference(x, L0_conv_theta_w, L0_conv_theta_b, L0_conv_phi_w, L0_conv_phi_b, L0_conv_W_w, L0_conv_W_b):
    import jax
    import jax.numpy as jnp
    def _L0_conv_ref(frame, theta_w, theta_b, phi_w, phi_b, W_w, W_b):
        import jax, jax.numpy as jnp
        import numpy as np
        C = 64

        def conv1x1(x, w, b):
            return jnp.einsum('bchw,oc->bohw', x, w) + b[None, :, None, None]
        B, Cc, H, Wd = frame.shape
        N = H * Wd
        x = conv1x1(frame, theta_w, theta_b).reshape(B, Cc, N).transpose(0, 2, 1)
        y = conv1x1(frame, phi_w, phi_b).reshape(B, Cc, N)
        scores = jnp.einsum('bnc,bcm->bnm', x, y)
        attn = jax.nn.softmax(scores, axis=1)
        z = jnp.einsum('bnm,bnc->bmc', attn.transpose(0, 2, 1).transpose(0, 2, 1), x)
        z = jnp.einsum('bnm,bmc->bnc', attn, x)
        z = z.transpose(0, 2, 1).reshape(B, Cc, H, Wd)
        return conv1x1(z, W_w, W_b)

    def _gn(v, G=32, eps=1e-5):
        B_, C_, H_, W_ = v.shape
        g = v.reshape(B_, G, C_ // G, H_, W_)
        m = jnp.mean(g, axis=(2, 3, 4), keepdims=True)
        s = jnp.var(g, axis=(2, 3, 4), keepdims=True)
        return ((g - m) / jnp.sqrt(s + eps)).reshape(v.shape)

    def _ln_c(v, eps=1e-6):
        m = jnp.mean(v, axis=1, keepdims=True)
        s = jnp.var(v, axis=1, keepdims=True)
        return (v - m) / jnp.sqrt(s + eps)

    def _ln_t(v, eps=1e-5):
        m = jnp.mean(v, axis=-1, keepdims=True)
        s = jnp.var(v, axis=-1, keepdims=True)
        return (v - m) / jnp.sqrt(s + eps)

    def _to_tokens(v):
        B_, C_, H_, W_ = v.shape
        return v.reshape(B_, C_, H_ * W_).transpose(0, 2, 1)
    def _from_tokens(t, like):
        B_, C_, H_, W_ = like.shape
        return t.transpose(0, 2, 1).reshape(B_, C_, H_, W_)

    x = x + _L0_conv_ref(_gn(x), L0_conv_theta_w, L0_conv_theta_b, L0_conv_phi_w, L0_conv_phi_b, L0_conv_W_w, L0_conv_W_b)
    return x


_drawn_inputs = setup_inputs


def setup_inputs(seed=0):
    import zlib

    import numpy as np

    out = dict(_drawn_inputs(seed))
    spreads = {}
    factors = {}
    for name, (base, spread) in spreads.items():
        noise = np.random.default_rng([zlib.crc32(name.encode()), seed]).standard_normal(out[name].shape)
        drawn = base * np.exp(spread * noise) if base else spread * noise
        out[name] = jnp.asarray(drawn.astype(out[name].dtype))
    for name, factor in factors.items():
        out[name] = (out[name] * factor).astype(out[name].dtype)
    return out
```

```python
from contextlib import ExitStack

import concourse.bass as bass
from concourse import mybir


F32 = mybir.dt.float32
F32R = mybir.dt.float32r
I32 = mybir.dt.int32
ACT = mybir.ActivationFunctionType
ALU = mybir.AluOpType
AX = mybir.AxisListType

NORM_GROUPS = 32
NORM_EPS = 1e-5
P = 128
HALF = 512
CHUNK = 2 * HALF
G = 3
RING = 3
PREPARE_AT = 2
LEAD = 2
RSQRT_GUESS = 0x5F3759DF
NEWTON_STEPS = 3


def attention_kernel(nc, x, theta_T2, theta, phi_T2, W_T, biases, norm_mean, out):
    B, C, N = x.shape
    NCH = N // CHUNK
    UNITS = NCH * G
    GROUPS = N // (P * G)
    TG = B * GROUPS
    GM = G * P
    USES = NCH + G
    assert C * 2 == P and N % CHUNK == 0 and N % GM == 0 and GROUPS % 2 == 0 and B == 2
    assert UNITS % RING == 0 and USES % 2 == 0 and NCH > PREPARE_AT + G

    with ExitStack() as ctx:
        def sb(name, shape, dt=F32):
            return ctx.enter_context(nc.sbuf_tensor(name, shape, dt))

        def sem(name):
            return ctx.enter_context(nc.semaphore(name))

        probs = sb("probs", [P, UNITS, CHUNK])
        x_parts = sb("x_parts", [P, N], F32R)
        acc = sb("acc", [P, NCH, HALF])
        y_high = sb("y_high", [P, 2, G, P], F32R)
        y_low = sb("y_low", [P, 2, G, P], F32R)
        v = sb("v", [P, 2, G, C])
        v_scaled = sb("v_scaled", [P, NCH, G, C])
        g_group = sb("g_group", [C, 2, GM])
        g_chunk = sb("g_chunk", [P, 2, HALF])
        theta_T2_sb = sb("theta_T2_sb", [P, P])
        theta_sb = sb("theta_sb", [C, C])
        phi_T2_sb = sb("phi_T2_sb", [C, P])
        W_T_sb = sb("W_T_sb", [C, C])
        biases_sb = sb("biases_sb", [P, 3])
        theta_b, phi_b, W_b = (biases_sb[:, k:k + 1] for k in range(3))
        norm_mean_sb = sb("norm_mean_sb", [P, P])
        theta_b_wide = sb("theta_b_wide", [C, P])
        WX_T = sb("WX_T", [C, C])
        v_bias = sb("v_bias", [P, C])
        neg_max = sb("neg_max", [P, 2, UNITS])
        neg_max_all = sb("neg_max_all", [P, G])
        max_diff = sb("max_diff", [P, UNITS])
        correction = sb("correction", [P, UNITS])
        chunk_sum = sb("chunk_sum", [P, UNITS])
        corrected_sum = sb("corrected_sum", [P, UNITS])
        total = sb("total", [P, G])
        inv_total = sb("inv_total", [P, G])
        factor = sb("factor", [P, NCH, G])
        bn = sb("bn", [P, NCH, 6])
        half_stat = sb("half_stat", [P, 2])
        mean = sb("mean", [P, B])
        rstd = sb("rstd", [P, B])
        spread = sb("spread", [P, 1])
        second = sb("second", [P, 1])
        variance = sb("variance", [P, 1])
        shifted = sb("shifted", [P, 1], I32)
        guess = sb("guess", [P, 1], I32)
        y0 = sb("y0", [P, 1])
        newton = sb("newton", [P, 1])

        ring = ctx.enter_context(nc.psum_tensor("ring", [P, RING, CHUNK], F32))
        zbank = ctx.enter_context(nc.psum_tensor("zbank", [P, 2, HALF], F32))

        weights_loaded = sem("weights_loaded")
        acc_loaded = [sem(f"acc_loaded{j}") for j in range(NCH)]
        x1_loaded = sem("x1_loaded")
        g_group_loaded = [sem(f"g_group_loaded{k}") for k in range(2)]
        g_chunk_loaded = [sem(f"g_chunk_loaded{k}") for k in range(2)]
        out_stored = sem("out_stored")
        wide_made = sem("wide_made")
        half_stat_made = sem("half_stat_made")
        zbank_full = sem("zbank_full")
        zbank_read = sem("zbank_read")
        dve_step = sem("dve_step")
        g_chunk_ready = sem("g_chunk_ready")
        g_group_ready = sem("g_group_ready")
        x_made = sem("x_made")
        x_rounded = sem("x_rounded")
        x_split = sem("x_split")
        y_split = sem("y_split")
        scores_made = sem("scores_made")
        max_taken = sem("max_taken")
        probs_made = sem("probs_made")
        diff_made = sem("diff_made")
        correction_made = sem("correction_made")
        factor_made = sem("factor_made")
        v_first = sem("v_first")
        v_rest = sem("v_rest")
        z_made = sem("z_made")

        x_halves = x.rearrange("b c (j h n) -> b h c j n", h=2, n=HALF)
        out_halves = out.rearrange("b c (j h n) -> b h c j n", h=2, n=HALF)
        X1_UNIT = UNITS - (NCH * HALF + CHUNK - 1) // CHUNK
        x1_raw = probs[:, X1_UNIT:, :].rearrange("p u n -> p (u n)")[:, 0:NCH * HALF].rearrange(
            "p (j n) -> p j n", n=HALF)

        SWAP = GROUPS - 1

        def ring_units(t_is_swap):
            units = []
            for k in range(UNITS):
                units.append(("s", k))
                if t_is_swap and k % G == G - 1:
                    units.append(("x", k // G))
            return units

        PLAIN, SWAPPING = ring_units(False), ring_units(True)
        FIRST = [("x", j) for j in range(NCH)]
        assert len(FIRST) % RING == 0 and len(SWAPPING) % RING == 0

        USE_STATS = (2, 4 + 2 * G)
        USE_PREP = (4, 4 + G)
        BEFORE = 6 + 2 * G
        assert BEFORE % 2 == 0

        def z_place(j):
            return j + min(max(j - PREPARE_AT, 0), G)

        def prep_place(b):
            return PREPARE_AT + 2 * b + 1

        def z_use(t, j):
            if isinstance(t, int) and t >= TG - 1:
                return BEFORE + (TG - 2) * USES + (t - TG + 1) * NCH + j
            return BEFORE + (t - 1) * USES + z_place(j)

        def prep_use(t, b):
            return USE_PREP[1] + b if isinstance(t, int) and t == 0 else BEFORE + (t - 1) * USES + prep_place(b)

        def z_bank(t, last, j):
            if last:
                return ((TG - 2) * USES + (t - TG + 1) * NCH + j) % 2
            return z_place(j) % 2

        def prep_bank(first, b):
            return (USE_PREP[1] + b) % 2 if first else prep_place(b) % 2

        def is_last(t):
            return isinstance(t, int) and t >= TG - 1

        def turns(engine, turn):
            for batch in range(B):
                t0 = batch * GROUPS
                turn(t0, 0)
                with engine.Fori(t0 + 1, t0 + GROUPS - 1, 2) as t:
                    turn(t, 1)
                    turn(t + 1, 0)
                turn(t0 + GROUPS - 1, 1)
            turn(TG, 0)

        block = ctx.enter_context(nc.Block())

        @block.sync
        def _(sp):
            for j in range(NCH):
                for h in range(2):
                    sp.dma_start(acc[h * C:(h + 1) * C, j, :], x_halves[0, h, :, j, :]).then_inc(acc_loaded[j], 16)
            for dst, src in ((norm_mean_sb, norm_mean), (theta_T2_sb, theta_T2), (theta_sb, theta),
                             (phi_T2_sb, phi_T2), (W_T_sb, W_T), (biases_sb, biases)):
                sp.dma_start(dst[:, :], src).then_inc(weights_loaded, 16)

            def load_group(batch, t, parity):
                m0 = (t - batch * GROUPS) * GM
                sp.dma_start(g_group[:, parity, :], x[batch, :, bass.ds(m0, GM)]).then_inc(g_group_loaded[parity], 16)

            load_group(0, 0, 0)
            load_group(0, 1, 1)
            for h in range(2):
                sp.dma_start(x1_raw[h * C:(h + 1) * C, :, :], x_halves[1, h, :, :, :]).then_inc(x1_loaded, 16)

            def turn(t, parity, batch):
                first = isinstance(t, int)
                if not first or t + 2 < TG:
                    sp.wait_ge(y_split, G * t + G)
                    load_group(batch, t + 2, parity)
                if first and t == SWAP:
                    for j in range(NCH):
                        if j >= 2:
                            sp.wait_ge(x_made, NCH + j - 1)
                        for h in range(2):
                            sp.dma_start(g_chunk[h * C:(h + 1) * C, j % 2, :],
                                         x_halves[1, h, :, j, :]).then_inc(g_chunk_loaded[j % 2], 16)
                if first and t in (GROUPS, TG):
                    done = (t // GROUPS - 1) * NCH
                    for j in range(NCH):
                        sp.wait_ge(zbank_read, z_use(t, j) + 1)
                        for h in range(2):
                            sp.dma_start(out_halves[t // GROUPS - 1, h, :, j, :],
                                         acc[h * C:(h + 1) * C, j, :]).then_inc(out_stored, 16)
                        if t == GROUPS:
                            sp.wait_ge(out_stored, 32 * (done + j + 1))
                            for h in range(2):
                                sp.dma_start(acc[h * C:(h + 1) * C, j, :],
                                             x_halves[1, h, :, j, :]).then_inc(acc_loaded[j], 16)

            for batch in range(B):
                t0 = batch * GROUPS
                turn(t0, 0, batch)
                with sp.Fori(t0 + 1, t0 + GROUPS - 3, 2) as t:
                    turn(t, 1, batch)
                    turn(t + 1, 0, batch)
                for t in range(t0 + GROUPS - 3, t0 + GROUPS):
                    turn(t, t % 2, (t + 2) // GROUPS)
            turn(TG, 0, None)
            sp.wait_ge(out_stored, 32 * B * NCH)

        @block.tensor
        def _(pe):
            def use_z_bank(use):
                if not isinstance(use, int) or use >= 2:
                    pe.wait_ge(zbank_read, use - 1)

            def free_ring_slot(t, units, before, at):
                if at >= RING:
                    kind, k = units[at - RING]
                    tt = t
                else:
                    kind, k = before[at - RING]
                    tt = t - 1
                if kind == "s":
                    pe.wait_ge(probs_made, UNITS * tt + k + 1)
                else:
                    pe.wait_ge(x_split, (0 if before is FIRST and at < RING else NCH) + k + 1)

            def x_chunk(batch, j, slot):
                pe.wait_ge(g_chunk_ready, batch * NCH + j + 1)
                for h in range(2):
                    last = nc.tensor.matmul(ring[:, slot, h * HALF:(h + 1) * HALF],
                                            theta_T2_sb[h * C:(h + 1) * C, :],
                                            g_chunk[h * C:(h + 1) * C, j % 2, :], start=True, stop=True)
                last.then_inc(x_made, 1)

            def scores(t, parity, k, swap, before):
                units = SWAPPING if swap else PLAIN
                at = units.index(("s", k))
                free_ring_slot(t, units, before, at)
                if k == 0:
                    pe.wait_ge(y_split, G * t + G)
                if isinstance(t, int) and t % GROUPS == 0 and k % G == 0:
                    pe.wait_ge(x_split, t // GROUPS * NCH + k // G + 1)
                j, b = k // G, k % G
                for part in (y_high, y_low):
                    for h in range(2):
                        n0 = j * CHUNK + h * HALF
                        last = nc.tensor.matmul(ring[:, at % RING, h * HALF:(h + 1) * HALF],
                                                part[:, parity, b, :], x_parts[:, n0:n0 + HALF],
                                                start=(part is y_high), stop=(part is y_low))
                last.then_inc(scores_made, 1)

            def z_step(t, k):
                j, b = k // G, k % G
                if k == 0:
                    pe.wait_ge(v_first, t)
                if j == 1 and b == 0:
                    pe.wait_ge(v_rest, 2 * t - 1)
                if j == G and b == 0:
                    pe.wait_ge(v_rest, 2 * t)
                if b == 0:
                    use_z_bank(z_use(t, j))
                bank = z_bank(t, is_last(t), j)
                for h in range(2):
                    last = nc.tensor.matmul(zbank[h * C:(h + 1) * C, bank, :], v_scaled[:, j, b, :],
                                            probs[:, k, h * HALF:(h + 1) * HALF],
                                            start=(b == 0), stop=(b == G - 1))
                last.then_inc(z_made, 1)

            def prepare(t_of, use, bank, parity, b):
                if b == 0:
                    pe.wait_ge(g_group_ready, t_of + 1)
                use_z_bank(use)
                g = g_group[:, parity, b * P:(b + 1) * P]
                nc.tensor.matmul(zbank[:, bank, 0:P], phi_T2_sb[:, :], g, start=True, stop=True)
                nc.tensor.matmul(zbank[:, bank, P:P + C], g, WX_T[:, :],
                                 start=True, stop=True).then_inc(zbank_full, 1)

            def norm_statistics(batch):
                for s in range(2):
                    pe.wait_ge(half_stat_made, 2 * batch + s + 1)
                    use = USE_STATS[batch] + s
                    use_z_bank(use)
                    nc.tensor.matmul(zbank[:, use % 2, 0:1], norm_mean_sb[:, :],
                                     (half_stat[:, 0:1], second[:, 0:1])[s], start=True, stop=True
                                     ).then_inc(zbank_full, 1)

            pe.wait_ge(weights_loaded, 16 * 6)
            nc.tensor.matmul(zbank[0:C, 0, 0:C], theta_sb[:, :], W_T_sb[:, :], start=True, stop=True
                             ).then_inc(zbank_full, 1)
            pe.wait_ge(wide_made, 1)
            nc.tensor.matmul(zbank[:, 1, 0:C], theta_b_wide[:, :], W_T_sb[:, :], start=True, stop=True
                             ).then_inc(zbank_full, 1)
            norm_statistics(0)
            for b in range(G):
                prepare(0, USE_PREP[0] + b, (USE_PREP[0] + b) % 2, 0, b)
            for j in range(NCH):
                if j >= RING:
                    pe.wait_ge(x_split, j - RING + 1)
                x_chunk(0, j, j % RING)
            for k in range(LEAD):
                scores(0, 0, k, False, FIRST)

            def turn(t, parity):
                fixed = isinstance(t, int)
                swap = fixed and t == SWAP
                before = FIRST if fixed and t == 0 else SWAPPING if fixed and t == SWAP + 1 else PLAIN
                for k in range(UNITS):
                    if not (fixed and t == 0):
                        z_step(t, k)
                    b = k // G - PREPARE_AT
                    if k % G == G - 1 and 0 <= b < G and not (fixed and t >= TG - 1):
                        prepare(t + 1, prep_use(t, b), prep_bank(fixed and t == 0, b), 1 - parity, b)
                    if fixed and t == 0 and k == G * (PREPARE_AT + G):
                        norm_statistics(1)
                    if fixed and t == TG:
                        continue
                    ahead = k + LEAD
                    if ahead < UNITS:
                        scores(t, parity, ahead, swap, before)
                        if swap and ahead % G == G - 1:
                            j = ahead // G
                            at = SWAPPING.index(("x", j))
                            free_ring_slot(t, SWAPPING, PLAIN, at)
                            x_chunk(1, j, at % RING)
                    elif not (fixed and t == TG - 1):
                        scores(t + 1, 1 - parity, ahead - UNITS, fixed and t + 1 == SWAP,
                               SWAPPING if swap else PLAIN)

            turns(pe, turn)

        @block.scalar
        def _(act):
            def round_x(batch, j, slot):
                act.wait_ge(x_made, batch * NCH + j + 1)
                if batch:
                    act.wait_ge(scores_made, UNITS * SWAP + G * j + G)
                nc.scalar.activation(x_parts[:, j * CHUNK:(j + 1) * CHUNK], ring[:, slot, :], ACT.Identity,
                                     bias=theta_b).then_inc(x_rounded, 1)

            act.wait_ge(weights_loaded, 16 * 6)
            for j in range(NCH):
                round_x(0, j, j % RING)

            def turn(t, parity):
                fixed = isinstance(t, int)
                if fixed and t == TG:
                    return
                swap = fixed and t == SWAP
                for at, (kind, k) in enumerate(SWAPPING if swap else PLAIN):
                    if kind == "x":
                        round_x(1, k, at % RING)
                        continue
                    act.wait_ge(max_taken, UNITS * t + k + 1)
                    if not (fixed and t == 0):
                        act.wait_ge(z_made, UNITS * (t - 1) + k + 1)
                    elif k == X1_UNIT:
                        act.wait_ge(half_stat_made, 3)
                    nc.scalar.activation(probs[:, k, :], ring[:, at % RING, :], ACT.Exp,
                                         bias=neg_max[:, parity, k:k + 1],
                                         accum_out=chunk_sum[:, k:k + 1]).then_inc(probs_made, 1)
                act.wait_ge(diff_made, t + 1)
                nc.scalar.activation(correction[:, :], max_diff[:, :], ACT.Exp).then_inc(correction_made, 1)

            turns(act, turn)

        @block.vector
        def _(dve):
            steps = [0]
            base = [0]

            def link(ins):
                steps[0] += 1
                ins.then_inc(dve_step, 1)
                dve.wait_ge(dve_step, base[0] + steps[0])

            def half_statistics(batch, src, arrived):
                for j in range(NCH):
                    arrived(j)
                    ins = nc.vector.bn_stats(bn[:, j, :], src[:, j, :])
                link(ins)
                ins = nc.vector.bn_aggr(half_stat[:, :], bn[:, :, :].rearrange("p j s -> p (j s)"))
                ins.then_inc(half_stat_made, 1)

            def statistics(batch):
                uses = USE_STATS[batch]
                full = 2 if batch == 0 else 4 + 2 * G
                dve.wait_ge(zbank_full, full + 1)
                nc.vector.tensor_copy(mean[:, batch:batch + 1], zbank[:, uses % 2, 0:1]).then_inc(zbank_read, 1)
                dve.wait_ge(zbank_read, uses + 1)
                dve.wait_ge(half_stat_made, 2 * batch + 1)
                link(nc.vector.tensor_tensor(spread[:, :], half_stat[:, 0:1], mean[:, batch:batch + 1], ALU.subtract))
                nc.vector.scalar_tensor_tensor(second[:, :], spread[:, :], spread[:, :], half_stat[:, 1:2],
                                               ALU.mult, ALU.add).then_inc(half_stat_made, 1)
                dve.wait_ge(zbank_full, full + 2)
                nc.vector.tensor_scalar(variance[:, :], zbank[:, (uses + 1) % 2, 0:1], NORM_EPS, None,
                                        ALU.add).then_inc(zbank_read, 1)
                dve.wait_ge(zbank_read, uses + 2)
                link(nc.vector.tensor_scalar(shifted[:, :], variance[:, :].bitcast(I32), 1, None,
                                             ALU.logical_shift_right))
                link(nc.vector.tensor_scalar(guess[:, :], shifted[:, :], -1.0, float(RSQRT_GUESS),
                                             ALU.mult, ALU.add))
                root = guess[:, :].bitcast(F32)
                for s in range(NEWTON_STEPS):
                    link(nc.vector.scalar_tensor_tensor(y0[:, :], root, variance[:, :], root, ALU.mult, ALU.mult))
                    link(nc.vector.tensor_scalar(newton[:, :], y0[:, :], -0.5, 1.5, ALU.mult, ALU.add))
                    to = rstd[:, batch:batch + 1] if s == NEWTON_STEPS - 1 else second[:, :]
                    link(nc.vector.tensor_tensor(to, root, newton[:, :], ALU.mult))
                    root = to

            def normalise(dst, src, batch, n):
                return nc.vector.tensor_scalar(dst, src, mean[0:n, batch:batch + 1], rstd[0:n, batch:batch + 1],
                                               ALU.subtract, ALU.mult)

            def split_x(batch, j, slot):
                dve.wait_ge(x_rounded, batch * NCH + j + 1)
                low = x_parts[C:P, j * CHUNK:(j + 1) * CHUNK]
                nc.vector.scalar_tensor_tensor(low, ring[C:P, slot, :], theta_b[C:P], low.bitcast(F32),
                                               ALU.add, ALU.subtract).then_inc(x_split, 1)

            def split_y(full, parity, bank, b):
                dve.wait_ge(zbank_full, full)
                high = y_high[:, parity, b, :]
                link(nc.vector.tensor_scalar(high, zbank[:, bank, 0:P], phi_b, None, ALU.add))
                nc.vector.scalar_tensor_tensor(y_low[:, parity, b, :], zbank[:, bank, 0:P], phi_b,
                                               high.bitcast(F32), ALU.add, ALU.subtract).then_inc(y_split, 1)
                nc.vector.tensor_tensor(v[:, parity, b, :], zbank[:, bank, P:P + C], v_bias[:, :],
                                        ALU.add).then_inc(zbank_read, 1)

            def add_z(t, j):
                fixed = isinstance(t, int)
                dve.wait_ge(z_made, UNITS * (t - 1) + G * j + G)
                dve.wait_ge(acc_loaded[j], 32 * (1 if now[0] <= GROUPS else 2))
                src = zbank[:, z_bank(t, is_last(t), j), :]
                if fixed and t % GROUPS == 0:
                    ins = nc.vector.scalar_tensor_tensor(acc[:, j, :], src, W_b, acc[:, j, :], ALU.add, ALU.add)
                else:
                    ins = nc.vector.tensor_tensor(acc[:, j, :], src, acc[:, j, :], ALU.add)
                ins.then_inc(zbank_read, 1)

            def take_max(t, parity, k, slot):
                dve.wait_ge(scores_made, UNITS * t + k + 1)
                nc.vector.tensor_reduce(neg_max[:, parity, k:k + 1], ring[:, slot, :], AX.X, ALU.max,
                                        negate=True).then_inc(max_taken, 1)

            def join_maxima(t, parity):
                dve.wait_ge(max_taken, UNITS * t + UNITS)
                link(nc.vector.tensor_reduce(neg_max_all[:, :], neg_max[:, parity, :].rearrange("p (j b) -> p b j", b=G),
                                             AX.X, ALU.min))
                nc.vector.tensor_tensor(max_diff[:, :].rearrange("p (j b) -> p j b", b=G),
                                        neg_max_all[:, :].unsqueeze(1).to_broadcast([P, NCH, G]),
                                        neg_max[:, parity, :].rearrange("p (j b) -> p j b", b=G),
                                        ALU.subtract).then_inc(diff_made, 1)

            def join_sums(t, parity):
                dve.wait_ge(correction_made, t + 1)
                link(nc.vector.tensor_tensor(corrected_sum[:, :], chunk_sum[:, :], correction[:, :], ALU.mult))
                link(nc.vector.tensor_reduce(total[:, :], corrected_sum[:, :].rearrange("p (j b) -> p b j", b=G),
                                             AX.X, ALU.add))
                link(nc.vector.reciprocal(inv_total[:, :], total[:, :]))
                nc.vector.tensor_tensor(factor[:, :, :], correction[:, :].rearrange("p (j b) -> p j b", b=G),
                                        inv_total[:, :].unsqueeze(1).to_broadcast([P, NCH, G]),
                                        ALU.mult).then_inc(factor_made, 1)
                dve.wait_ge(factor_made, t + 1)
                nc.vector.tensor_tensor(v_scaled[:, 0, :, :], v[:, parity, :, :],
                                        factor[:, 0, :].unsqueeze(2).to_broadcast([P, G, C]),
                                        ALU.mult).then_inc(v_first, 1)

            dve.wait_ge(weights_loaded, 16 * 6)
            nc.vector.tensor_copy(theta_b_wide[:, :], theta_b[0:C].to_broadcast([C, P])).then_inc(wide_made, 1)
            half_statistics(0, acc, lambda j: dve.wait_ge(acc_loaded[j], 32))
            dve.wait_ge(zbank_full, 1)
            nc.vector.tensor_copy(WX_T[:, :], zbank[0:C, 0, 0:C]).then_inc(zbank_read, 1)
            dve.wait_ge(zbank_full, 2)
            nc.vector.tensor_copy(v_bias[:, :], zbank[:, 1, 0:C]).then_inc(zbank_read, 1)
            statistics(0)

            def normalise_group(t, parity, batch):
                if isinstance(t, int):
                    loads = t // 2 + 1
                    dve.wait_ge(g_group_loaded[parity], 16 * loads)
                else:
                    dve.wait_ge(g_group_loaded[parity], 8 * (t + (2 - parity)))
                normalise(g_group[:, parity, :], g_group[:, parity, :], batch, C).then_inc(g_group_ready, 1)

            normalise_group(0, 0, 0)
            for j in range(2):
                normalise(g_chunk[:, j % 2, :], acc[:, j, :], 0, P).then_inc(g_chunk_ready, 1)
            for b in range(G):
                split_y(4 + b + 1, 0, (USE_PREP[0] + b) % 2, b)
            for j in range(NCH):
                split_x(0, j, j % RING)
                if j + 2 < NCH:
                    normalise(g_chunk[:, j % 2, :], acc[:, j + 2, :], 0, P).then_inc(g_chunk_ready, 1)
            for k in range(LEAD):
                take_max(0, 0, k, k)

            now = [0]

            def turn(t, parity):
                fixed = isinstance(t, int)
                first, swap, last = fixed and t == 0, fixed and t == SWAP, fixed and t == TG - 1
                units = SWAPPING if swap else PLAIN
                for k in range(UNITS):
                    j, b = k // G, k % G
                    if k == 0 and not (fixed and t >= TG - 1):
                        normalise_group(t + 1, 1 - parity, 0 if now[0] + 1 < GROUPS else 1)
                    if swap and k % G == 0:
                        dve.wait_ge(g_chunk_loaded[j % 2], 32 * (j // 2 + 1))
                        normalise(g_chunk[:, j % 2, :], g_chunk[:, j % 2, :], 1, P).then_inc(g_chunk_ready, 1)
                    if k == UNITS - 1 and not (fixed and t == TG):
                        join_sums(t, parity)
                    if b == G - 1 and not first:
                        add_z(t, j)
                    prepared = j - PREPARE_AT
                    if b == G - 1 and 0 <= prepared < G and not (fixed and t >= TG - 1):
                        full = (4 if first else 6) + G * (t + 1) + prepared + 1
                        if prepared == 0 and not first:
                            dve.wait_ge(v_rest, 2 * t)
                        split_y(full, 1 - parity, prep_bank(first, prepared), prepared)
                    if first and k == G * (PREPARE_AT + G) - G:
                        half_statistics(1, x1_raw, lambda j: dve.wait_ge(x1_loaded, 32))
                    if first and k == G * (PREPARE_AT + G):
                        statistics(1)
                    if fixed and t == TG:
                        continue
                    ahead = k + LEAD
                    if ahead < UNITS:
                        take_max(t, parity, ahead, units.index(("s", ahead)) % RING)
                        if swap and ahead % G == 0:
                            split_x(1, ahead // G - 1, units.index(("x", ahead // G - 1)) % RING)
                        if ahead == UNITS - 1:
                            join_maxima(t, parity)
                            if swap:
                                split_x(1, NCH - 1, units.index(("x", NCH - 1)) % RING)
                    elif not last:
                        take_max(t + 1, 1 - parity, ahead - UNITS, (ahead - UNITS) % RING)

            for batch in range(B):
                t0 = batch * GROUPS
                now[0] = t0
                turn(t0, 0)
                start, steps[0] = base[0] + steps[0], 0
                with dve.Fori(t0 + 1, t0 + GROUPS - 1, 2) as t:
                    now[0] = t0 + 1
                    per_turn = G + 4
                    base[0] = (t - (t0 + 1)) * per_turn + start
                    turn(t, 1)
                    turn(t + 1, 0)
                    assert steps[0] == 2 * per_turn
                base[0], steps[0] = start + (GROUPS - 2) * per_turn, 0
                now[0] = t0 + GROUPS - 1
                turn(now[0], 1)
            now[0] = TG
            turn(TG, 0)

        @block.gpsimd
        def _(pool):
            def turn(t, parity):
                if isinstance(t, int) and t == TG:
                    return
                pool.wait_ge(factor_made, t + 1)
                if not (isinstance(t, int) and t == 0):
                    pool.wait_ge(z_made, UNITS * t)
                for j0, j1 in ((1, G), (G, NCH)):
                    nc.gpsimd.tensor_tensor(v_scaled[:, j0:j1, :, :],
                                            v[:, parity, :, :].unsqueeze(1).to_broadcast([P, j1 - j0, G, C]),
                                            factor[:, j0:j1, :].unsqueeze(3).to_broadcast([P, j1 - j0, G, C]),
                                            ALU.mult).then_inc(v_rest, 1)

            turns(pool, turn)


def kernel(x, L0_conv_theta_w, L0_conv_theta_b, L0_conv_phi_w, L0_conv_phi_b, L0_conv_W_w, L0_conv_W_b):
    import numpy as np
    import concourse.bacc as bacc
    from concourse.bass_utils import run_bass_kernel_spmd as run

    x = np.asarray(x)
    B, C, H, W = x.shape
    channel = np.arange(2 * C) % C
    per_group = C // NORM_GROUPS
    same = channel[:, None] // per_group == channel[None, :] // per_group
    arrays = {
        "x": np.ascontiguousarray(x.reshape(B, C, H * W)),
        "theta_T2": np.ascontiguousarray(np.tile(np.asarray(L0_conv_theta_w).T, (2, 2))),
        "theta": np.ascontiguousarray(np.asarray(L0_conv_theta_w)),
        "phi_T2": np.ascontiguousarray(np.tile(np.asarray(L0_conv_phi_w).T, (1, 2))),
        "W_T": np.ascontiguousarray(np.asarray(L0_conv_W_w).T),
        "biases": np.ascontiguousarray(np.stack(
            [np.tile(np.asarray(b), 2) for b in (L0_conv_theta_b, L0_conv_phi_b, L0_conv_W_b)], axis=1)),
        "norm_mean": np.where(same, np.float32(1 / (2 * per_group)), np.float32(0)),
    }
    nc = bacc.Bacc("TRN2", target_bir_lowering=False, num_devices=1)
    args = [nc.dram_tensor(name, a.shape, mybir.dt.from_np(a.dtype), kind="ExternalInput").ap()
            for name, a in arrays.items()]
    out = nc.dram_tensor("out", (B, C, H * W), F32, kind="ExternalOutput").ap()
    attention_kernel(nc, *args, out)
    result = run(nc, [arrays], core_ids=[0])
    return result.results[0]["out"].reshape(B, C, H, W)
```

```python
from contextlib import ExitStack

import concourse.bass as bass
from concourse import mybir


F32 = mybir.dt.float32
F32R = mybir.dt.float32r
I32 = mybir.dt.int32
ACT = mybir.ActivationFunctionType
ALU = mybir.AluOpType
AX = mybir.AxisListType

NORM_GROUPS = 32
NORM_EPS = 1e-5
P = 128
HALF = 512
CHUNK = 2 * HALF
G = 3
RING = 3
PREPARE_AT = 2
RSQRT_GUESS = 0x5F3759DF
NEWTON_STEPS = 3


def attention_kernel(nc, x, theta_T2, theta2, phi_T2, W_T, biases, norm_mean, out):
    B, C, N = x.shape
    NCH = N // CHUNK
    UNITS = NCH * G
    GROUPS = N // (P * G)
    TG = B * GROUPS
    GM = G * P
    USES = NCH + G
    assert C * 2 == P and N % CHUNK == 0 and N % GM == 0 and GROUPS % 2 == 0 and B == 2
    assert UNITS % RING == 0 and USES % 2 == 0 and NCH > PREPARE_AT + G

    with ExitStack() as ctx:
        def sb(name, shape, dt=F32):
            return ctx.enter_context(nc.sbuf_tensor(name, shape, dt))

        def sem(name):
            return ctx.enter_context(nc.semaphore(name))

        probs = sb("probs", [P, UNITS, CHUNK])
        x_parts = sb("x_parts", [P, N], F32R)
        acc = sb("acc", [P, NCH, HALF])
        y_high = sb("y_high", [P, 2, G, P], F32R)
        y_low = sb("y_low", [P, 2, G, P], F32R)
        v = sb("v", [P, 2, G, C])
        v_scaled = sb("v_scaled", [P, NCH, G, C])
        x_group = sb("x_group", [P, 2, GM])
        g_parts = sb("g_parts", [P, 2, GM], F32R)
        g_chunk = sb("g_chunk", [P, 2, HALF])
        theta_half = sb("theta_half", [P, 2, P])
        theta2_sb = sb("theta2_sb", [C, P])
        phi_T2_sb = sb("phi_T2_sb", [P, P])
        phi_high = sb("phi_high", [P, P], F32R)
        phi_low = sb("phi_low", [P, P], F32R)
        W_T_sb = sb("W_T_sb", [C, C])
        biases_sb = sb("biases_sb", [P, 3])
        theta_b, phi_b, W_b = (biases_sb[:, k:k + 1] for k in range(3))
        norm_mean_sb = sb("norm_mean_sb", [P, P])
        theta_b_wide = sb("theta_b_wide", [C, P])
        WX_T = sb("WX_T", [P, C])
        WX_high = sb("WX_high", [P, C], F32R)
        WX_low = sb("WX_low", [P, C], F32R)
        v_bias = sb("v_bias", [P, C])
        neg_max = sb("neg_max", [P, 2, UNITS])
        neg_max_all = sb("neg_max_all", [P, G])
        max_diff = sb("max_diff", [P, UNITS])
        correction = sb("correction", [P, UNITS])
        chunk_sum = sb("chunk_sum", [P, UNITS])
        corrected_sum = sb("corrected_sum", [P, UNITS])
        total = sb("total", [P, G])
        inv_total = sb("inv_total", [P, G])
        factor = sb("factor", [P, NCH, G])
        bn = sb("bn", [P, NCH, 6])
        half_stat = sb("half_stat", [P, 2])
        mean = sb("mean", [P, B])
        rstd = sb("rstd", [P, B])
        spread = sb("spread", [P, 1])
        second = sb("second", [P, 1])
        variance = sb("variance", [P, 1])
        shifted = sb("shifted", [P, 1], I32)
        guess = sb("guess", [P, 1], I32)
        y0 = sb("y0", [P, 1])
        newton = sb("newton", [P, 1])

        ring = ctx.enter_context(nc.psum_tensor("ring", [P, RING, CHUNK], F32))
        zbank = ctx.enter_context(nc.psum_tensor("zbank", [P, 2, HALF], F32))

        weights_loaded = sem("weights_loaded")
        acc_loaded = [sem(f"acc_loaded{j}") for j in range(NCH)]
        x1_loaded = sem("x1_loaded")
        x_group_loaded = [sem(f"x_group_loaded{k}") for k in range(2)]
        g_chunk_loaded = [sem(f"g_chunk_loaded{k}") for k in range(2)]
        out_stored = sem("out_stored")
        zeros_made = sem("zeros_made")
        wide_made = sem("wide_made")
        weights_split = sem("weights_split")
        half_stat_made = sem("half_stat_made")
        zbank_full = sem("zbank_full")
        zbank_read = sem("zbank_read")
        dve_step = sem("dve_step")
        g_chunk_ready = sem("g_chunk_ready")
        g_group_ready = sem("g_group_ready")
        x_made = sem("x_made")
        x_rounded = sem("x_rounded")
        x_split = sem("x_split")
        y_split = sem("y_split")
        scores_made = sem("scores_made")
        max_taken = sem("max_taken")
        probs_made = sem("probs_made")
        diff_made = sem("diff_made")
        correction_made = sem("correction_made")
        factor_made = sem("factor_made")
        v_first = sem("v_first")
        v_rest = sem("v_rest")
        z_made = sem("z_made")

        x_halves = x.rearrange("b c (j h n) -> b h c j n", h=2, n=HALF)
        out_halves = out.rearrange("b c (j h n) -> b h c j n", h=2, n=HALF)
        X1_UNIT = UNITS - (NCH * HALF + CHUNK - 1) // CHUNK
        x1_raw = probs[:, X1_UNIT:, :].rearrange("p u n -> p (u n)")[:, 0:NCH * HALF].rearrange(
            "p (j n) -> p j n", n=HALF)

        SWAP = GROUPS - 1

        def ring_units(t_is_swap):
            units = []
            for k in range(UNITS):
                units.append(("s", k))
                if t_is_swap and k % G == G - 1:
                    units.append(("x", k // G))
            return units

        PLAIN, SWAPPING = ring_units(False), ring_units(True)
        FIRST = [("x", j) for j in range(NCH)]
        assert len(FIRST) % RING == 0 and len(SWAPPING) % RING == 0

        USE_STATS = (2, 4 + 2 * G)
        USE_PREP = (4, 4 + G)
        BEFORE = 6 + 2 * G
        assert BEFORE % 2 == 0

        def z_place(j):
            return j + min(max(j - PREPARE_AT, 0), G)

        def prep_place(b):
            return PREPARE_AT + 2 * b + 1

        def z_use(t, j):
            if isinstance(t, int) and t >= TG - 1:
                return BEFORE + (TG - 2) * USES + (t - TG + 1) * NCH + j
            return BEFORE + (t - 1) * USES + z_place(j)

        def prep_use(t, b):
            return USE_PREP[1] + b if isinstance(t, int) and t == 0 else BEFORE + (t - 1) * USES + prep_place(b)

        def z_bank(t, last, j):
            if last:
                return ((TG - 2) * USES + (t - TG + 1) * NCH + j) % 2
            return z_place(j) % 2

        def prep_bank(first, b):
            return (USE_PREP[1] + b) % 2 if first else prep_place(b) % 2

        def is_last(t):
            return isinstance(t, int) and t >= TG - 1

        def turns(engine, turn):
            for batch in range(B):
                t0 = batch * GROUPS
                turn(t0, 0)
                with engine.Fori(t0 + 1, t0 + GROUPS - 1, 2) as t:
                    turn(t, 1)
                    turn(t + 1, 0)
                turn(t0 + GROUPS - 1, 1)
            turn(TG, 0)

        block = ctx.enter_context(nc.Block())

        @block.sync
        def _(sp):
            for j in range(NCH):
                sp.dma_start(acc[0:C, j, :], x_halves[0, 0, :, j, :]).then_inc(acc_loaded[j], 16)

            def load_group(batch, t, parity):
                m0 = (t - batch * GROUPS) * GM
                for h in range(2):
                    sp.dma_start(x_group[h * C:(h + 1) * C, parity, :],
                                 x[batch, :, bass.ds(m0, GM)]).then_inc(x_group_loaded[parity], 16)

            load_group(0, 0, 0)
            load_group(0, 1, 1)
            for h in range(2):
                sp.dma_start(x1_raw[h * C:(h + 1) * C, :, :], x_halves[1, h, :, :, :]).then_inc(x1_loaded, 16)

            def turn(t, parity, batch):
                first = isinstance(t, int)
                if not first or t + 2 < TG:
                    sp.wait_ge(g_group_ready, t + 1)
                    load_group(batch, t + 2, parity)
                if first and t == SWAP:
                    for j in range(NCH):
                        if j >= 2:
                            sp.wait_ge(x_made, NCH + j - 1)
                        for h in range(2):
                            sp.dma_start(g_chunk[h * C:(h + 1) * C, j % 2, :],
                                         x_halves[1, h, :, j, :]).then_inc(g_chunk_loaded[j % 2], 16)
                if first and t in (GROUPS, TG):
                    done = (t // GROUPS - 1) * NCH
                    for j in range(NCH):
                        sp.wait_ge(zbank_read, z_use(t, j) + 1)
                        for h in range(2):
                            sp.dma_start(out_halves[t // GROUPS - 1, h, :, j, :],
                                         acc[h * C:(h + 1) * C, j, :]).then_inc(out_stored, 16)
                        if t == GROUPS:
                            sp.wait_ge(out_stored, 32 * (done + j + 1))
                            for h in range(2):
                                sp.dma_start(acc[h * C:(h + 1) * C, j, :],
                                             x_halves[1, h, :, j, :]).then_inc(acc_loaded[j], 16)

            for batch in range(B):
                t0 = batch * GROUPS
                turn(t0, 0, batch)
                with sp.Fori(t0 + 1, t0 + GROUPS - 3, 2) as t:
                    turn(t, 1, batch)
                    turn(t + 1, 0, batch)
                for t in range(t0 + GROUPS - 3, t0 + GROUPS):
                    turn(t, t % 2, (t + 2) // GROUPS)
            turn(TG, 0, None)
            sp.wait_ge(out_stored, 32 * B * NCH)

        @block.tensor
        def _(pe):
            def use_z_bank(use):
                if not isinstance(use, int) or use >= 2:
                    pe.wait_ge(zbank_read, use - 1)

            def free_ring_slot(t, units, before, at):
                if at >= RING:
                    kind, k = units[at - RING]
                    tt = t
                else:
                    kind, k = before[at - RING]
                    tt = t - 1
                if kind == "s":
                    pe.wait_ge(probs_made, UNITS * tt + k + 1)
                else:
                    pe.wait_ge(x_split, (0 if before is FIRST and at < RING else NCH) + k + 1)

            def x_chunk(batch, j, slot):
                pe.wait_ge(g_chunk_ready, batch * NCH + j + 1)
                for h in range(2):
                    last = nc.tensor.matmul(ring[:, slot, h * HALF:(h + 1) * HALF], theta_half[:, h, :],
                                            g_chunk[:, j % 2, :], start=True, stop=True)
                last.then_inc(x_made, 1)

            def scores(t, parity, k, swap, before):
                units = SWAPPING if swap else PLAIN
                at = units.index(("s", k))
                free_ring_slot(t, units, before, at)
                if k == 0:
                    pe.wait_ge(y_split, G * t + G)
                if isinstance(t, int) and t % GROUPS == 0 and k % G == 0:
                    pe.wait_ge(x_split, t // GROUPS * NCH + k // G + 1)
                j, b = k // G, k % G
                for part in (y_high, y_low):
                    for h in range(2):
                        n0 = j * CHUNK + h * HALF
                        last = nc.tensor.matmul(ring[:, at % RING, h * HALF:(h + 1) * HALF],
                                                part[:, parity, b, :], x_parts[:, n0:n0 + HALF],
                                                start=(part is y_high), stop=(part is y_low))
                last.then_inc(scores_made, 1)

            def z_step(t, k):
                j, b = k // G, k % G
                if k == 0:
                    pe.wait_ge(v_first, t)
                if j == 1 and b == 0:
                    pe.wait_ge(v_rest, 2 * t - 1)
                if j == G and b == 0:
                    pe.wait_ge(v_rest, 2 * t)
                if b == 0:
                    use_z_bank(z_use(t, j))
                bank = z_bank(t, is_last(t), j)
                for h in range(2):
                    last = nc.tensor.matmul(zbank[h * C:(h + 1) * C, bank, :], v_scaled[:, j, b, :],
                                            probs[:, k, h * HALF:(h + 1) * HALF],
                                            start=(b == 0), stop=(b == G - 1))
                last.then_inc(z_made, 1)

            def prepare(t_of, use, bank, parity, b):
                if b == 0:
                    pe.wait_ge(g_group_ready, t_of + 1)
                use_z_bank(use)
                g = g_parts[:, parity, b * P:(b + 1) * P]
                nc.tensor.matmul(zbank[:, bank, 0:P], phi_high[:, :], g, start=True, stop=False)
                nc.tensor.matmul(zbank[:, bank, 0:P], phi_low[:, :], g, start=False, stop=True)
                nc.tensor.matmul(zbank[:, bank, P:P + C], g, WX_high[:, :], start=True, stop=False)
                nc.tensor.matmul(zbank[:, bank, P:P + C], g, WX_low[:, :],
                                 start=False, stop=True).then_inc(zbank_full, 1)

            def norm_statistics(batch):
                for s in range(2):
                    pe.wait_ge(half_stat_made, 2 * batch + s + 1)
                    use = USE_STATS[batch] + s
                    use_z_bank(use)
                    nc.tensor.matmul(zbank[:, use % 2, 0:1], norm_mean_sb[:, :],
                                     (half_stat[:, 0:1], second[:, 0:1])[s], start=True, stop=True
                                     ).then_inc(zbank_full, 1)

            pe.wait_ge(weights_loaded, 16 * 7)
            nc.tensor.matmul(zbank[:, 0, 0:C], theta2_sb[:, :], W_T_sb[:, :], start=True, stop=True
                             ).then_inc(zbank_full, 1)
            pe.wait_ge(wide_made, 1)
            nc.tensor.matmul(zbank[:, 1, 0:C], theta_b_wide[:, :], W_T_sb[:, :], start=True, stop=True
                             ).then_inc(zbank_full, 1)
            norm_statistics(0)
            pe.wait_ge(weights_split, 2)
            for b in range(G):
                prepare(0, USE_PREP[0] + b, (USE_PREP[0] + b) % 2, 0, b)
            for j in range(NCH):
                if j >= RING:
                    pe.wait_ge(x_split, j - RING + 1)
                x_chunk(0, j, j % RING)
            for k in range(G):
                scores(0, 0, k, False, FIRST)

            def turn(t, parity):
                fixed = isinstance(t, int)
                swap = fixed and t == SWAP
                before = FIRST if fixed and t == 0 else SWAPPING if fixed and t == SWAP + 1 else PLAIN
                for j in range(NCH):
                    if not (fixed and t == 0):
                        for k in range(G * j, G * j + G):
                            z_step(t, k)
                    b = j - PREPARE_AT
                    if 0 <= b < G and not (fixed and t >= TG - 1):
                        prepare(t + 1, prep_use(t, b), prep_bank(fixed and t == 0, b), 1 - parity, b)
                    if fixed and t == 0 and j == PREPARE_AT + G:
                        norm_statistics(1)
                    if swap:
                        at = SWAPPING.index(("x", j))
                        free_ring_slot(t, SWAPPING, PLAIN, at)
                        x_chunk(1, j, at % RING)
                    for k in range(G * j + G, G * j + 2 * G):
                        if k < UNITS and not (fixed and t == TG):
                            scores(t, parity, k, swap, before)
                        if k >= UNITS and not (fixed and t >= TG - 1):
                            scores(t + 1, 1 - parity, k - UNITS, fixed and t + 1 == SWAP,
                                   SWAPPING if swap else PLAIN)

            turns(pe, turn)

        @block.scalar
        def _(act):
            def round_x(batch, j, slot):
                act.wait_ge(x_made, batch * NCH + j + 1)
                if batch:
                    act.wait_ge(scores_made, UNITS * SWAP + G * j + G)
                nc.scalar.activation(x_parts[:, j * CHUNK:(j + 1) * CHUNK], ring[:, slot, :], ACT.Identity,
                                     bias=theta_b).then_inc(x_rounded, 1)

            for j in range(NCH):
                act.dma_start(acc[C:P, j, :], x_halves[0, 1, :, j, :]).then_inc(acc_loaded[j], 16)
            act.wait_ge(weights_loaded, 16 * 7)
            for j in range(NCH):
                round_x(0, j, j % RING)

            def turn(t, parity):
                fixed = isinstance(t, int)
                if fixed and t == TG:
                    return
                swap = fixed and t == SWAP
                for at, (kind, k) in enumerate(SWAPPING if swap else PLAIN):
                    if kind == "x":
                        round_x(1, k, at % RING)
                        continue
                    act.wait_ge(max_taken, UNITS * t + k + 1)
                    if not (fixed and t == 0):
                        act.wait_ge(z_made, UNITS * (t - 1) + k + 1)
                    elif k == X1_UNIT:
                        act.wait_ge(half_stat_made, 3)
                    nc.scalar.activation(probs[:, k, :], ring[:, at % RING, :], ACT.Exp,
                                         bias=neg_max[:, parity, k:k + 1],
                                         accum_out=chunk_sum[:, k:k + 1]).then_inc(probs_made, 1)
                act.wait_ge(diff_made, t + 1)
                nc.scalar.activation(correction[:, :], max_diff[:, :], ACT.Exp).then_inc(correction_made, 1)

            turns(act, turn)

        @block.vector
        def _(dve):
            steps = [0]
            base = [0]

            def link(ins):
                steps[0] += 1
                ins.then_inc(dve_step, 1)
                dve.wait_ge(dve_step, base[0] + steps[0])

            def half_statistics(batch, src, arrived):
                for j in range(NCH):
                    arrived(j)
                    ins = nc.vector.bn_stats(bn[:, j, :], src[:, j, :])
                link(ins)
                ins = nc.vector.bn_aggr(half_stat[:, :], bn[:, :, :].rearrange("p j s -> p (j s)"))
                ins.then_inc(half_stat_made, 1)

            def statistics(batch):
                uses = USE_STATS[batch]
                full = 2 if batch == 0 else 4 + 2 * G
                dve.wait_ge(zbank_full, full + 1)
                nc.vector.tensor_copy(mean[:, batch:batch + 1], zbank[:, uses % 2, 0:1]).then_inc(zbank_read, 1)
                dve.wait_ge(zbank_read, uses + 1)
                dve.wait_ge(half_stat_made, 2 * batch + 1)
                link(nc.vector.tensor_tensor(spread[:, :], half_stat[:, 0:1], mean[:, batch:batch + 1], ALU.subtract))
                nc.vector.scalar_tensor_tensor(second[:, :], spread[:, :], spread[:, :], half_stat[:, 1:2],
                                               ALU.mult, ALU.add).then_inc(half_stat_made, 1)
                dve.wait_ge(zbank_full, full + 2)
                nc.vector.tensor_scalar(variance[:, :], zbank[:, (uses + 1) % 2, 0:1], NORM_EPS, None,
                                        ALU.add).then_inc(zbank_read, 1)
                dve.wait_ge(zbank_read, uses + 2)
                link(nc.vector.tensor_scalar(shifted[:, :], variance[:, :].bitcast(I32), 1, None,
                                             ALU.logical_shift_right))
                link(nc.vector.tensor_scalar(guess[:, :], shifted[:, :], -1.0, float(RSQRT_GUESS),
                                             ALU.mult, ALU.add))
                root = guess[:, :].bitcast(F32)
                for s in range(NEWTON_STEPS):
                    link(nc.vector.scalar_tensor_tensor(y0[:, :], root, variance[:, :], root, ALU.mult, ALU.mult))
                    link(nc.vector.tensor_scalar(newton[:, :], y0[:, :], -0.5, 1.5, ALU.mult, ALU.add))
                    to = rstd[:, batch:batch + 1] if s == NEWTON_STEPS - 1 else second[:, :]
                    link(nc.vector.tensor_tensor(to, root, newton[:, :], ALU.mult))
                    root = to

            def normalise(dst, src, batch, p0=0, p1=P):
                return nc.vector.tensor_scalar(dst, src, mean[p0:p1, batch:batch + 1], rstd[p0:p1, batch:batch + 1],
                                               ALU.subtract, ALU.mult)

            def split_x(batch, j, slot):
                dve.wait_ge(x_rounded, batch * NCH + j + 1)
                low = x_parts[C:P, j * CHUNK:(j + 1) * CHUNK]
                nc.vector.scalar_tensor_tensor(low, ring[C:P, slot, :], theta_b[C:P], low.bitcast(F32),
                                               ALU.add, ALU.subtract).then_inc(x_split, 1)

            def split_y(full, parity, bank, b):
                dve.wait_ge(zbank_full, full)
                high = y_high[:, parity, b, :]
                link(nc.vector.tensor_scalar(high, zbank[:, bank, 0:P], phi_b, None, ALU.add))
                nc.vector.scalar_tensor_tensor(y_low[:, parity, b, :], zbank[:, bank, 0:P], phi_b,
                                               high.bitcast(F32), ALU.add, ALU.subtract).then_inc(y_split, 1)
                nc.vector.tensor_tensor(v[:, parity, b, :], zbank[:, bank, P:P + C], v_bias[:, :],
                                        ALU.add).then_inc(zbank_read, 1)

            def add_z(t, j):
                fixed = isinstance(t, int)
                dve.wait_ge(z_made, UNITS * (t - 1) + G * j + G)
                dve.wait_ge(acc_loaded[j], 32 * (1 if now[0] <= GROUPS else 2))
                src = zbank[:, z_bank(t, is_last(t), j), :]
                if fixed and t % GROUPS == 0:
                    ins = nc.vector.scalar_tensor_tensor(acc[:, j, :], src, W_b, acc[:, j, :], ALU.add, ALU.add)
                else:
                    ins = nc.vector.tensor_tensor(acc[:, j, :], src, acc[:, j, :], ALU.add)
                ins.then_inc(zbank_read, 1)

            def take_max(t, parity, k, slot):
                dve.wait_ge(scores_made, UNITS * t + k + 1)
                nc.vector.tensor_reduce(neg_max[:, parity, k:k + 1], ring[:, slot, :], AX.X, ALU.max,
                                        negate=True).then_inc(max_taken, 1)

            def join_maxima(t, parity):
                dve.wait_ge(max_taken, UNITS * t + UNITS)
                link(nc.vector.tensor_reduce(neg_max_all[:, :], neg_max[:, parity, :].rearrange("p (j b) -> p b j", b=G),
                                             AX.X, ALU.min))
                nc.vector.tensor_tensor(max_diff[:, :].rearrange("p (j b) -> p j b", b=G),
                                        neg_max_all[:, :].unsqueeze(1).to_broadcast([P, NCH, G]),
                                        neg_max[:, parity, :].rearrange("p (j b) -> p j b", b=G),
                                        ALU.subtract).then_inc(diff_made, 1)

            def join_sums(t, parity):
                dve.wait_ge(correction_made, t + 1)
                link(nc.vector.tensor_tensor(corrected_sum[:, :], chunk_sum[:, :], correction[:, :], ALU.mult))
                link(nc.vector.tensor_reduce(total[:, :], corrected_sum[:, :].rearrange("p (j b) -> p b j", b=G),
                                             AX.X, ALU.add))
                link(nc.vector.reciprocal(inv_total[:, :], total[:, :]))
                nc.vector.tensor_tensor(factor[:, :, :], correction[:, :].rearrange("p (j b) -> p j b", b=G),
                                        inv_total[:, :].unsqueeze(1).to_broadcast([P, NCH, G]),
                                        ALU.mult).then_inc(factor_made, 1)
                dve.wait_ge(factor_made, t + 1)
                nc.vector.tensor_tensor(v_scaled[:, 0, :, :], v[:, parity, :, :],
                                        factor[:, 0, :].unsqueeze(2).to_broadcast([P, G, C]),
                                        ALU.mult).then_inc(v_first, 1)

            nc.vector.memset(theta_half[:, :, :], 0.0).then_inc(zeros_made, 1)
            dve.wait_ge(weights_loaded, 16 * 7)
            nc.vector.tensor_copy(theta_b_wide[:, :], theta_b[0:C].to_broadcast([C, P])).then_inc(wide_made, 1)
            half_statistics(0, acc, lambda j: dve.wait_ge(acc_loaded[j], 32))
            dve.wait_ge(zbank_full, 1)
            nc.vector.tensor_copy(WX_T[:, :], zbank[:, 0, 0:C]).then_inc(zbank_read, 1)
            dve.wait_ge(zbank_read, 1)
            for whole, high, low in ((WX_T, WX_high, WX_low), (phi_T2_sb, phi_high, phi_low)):
                link(nc.vector.tensor_copy(high[:, :], whole[:, :]))
                nc.vector.tensor_tensor(low[:, :], whole[:, :], high[:, :].bitcast(F32),
                                        ALU.subtract).then_inc(weights_split, 1)
            dve.wait_ge(zbank_full, 2)
            nc.vector.tensor_copy(v_bias[:, :], zbank[:, 1, 0:C]).then_inc(zbank_read, 1)
            statistics(0)

            def normalise_group(t, parity, batch):
                loads = 32 * (t // 2 + 1) if isinstance(t, int) else 16 * (t + (2 - parity))
                dve.wait_ge(x_group_loaded[parity], loads)
                link(normalise(g_parts[:, parity, :], x_group[:, parity, :], batch, 0, P))
                lower = x_group[C:P, parity, :]
                link(normalise(lower, lower, batch, C, P))
                low = g_parts[C:P, parity, :]
                nc.vector.tensor_tensor(low, lower, low.bitcast(F32), ALU.subtract).then_inc(g_group_ready, 1)

            normalise_group(0, 0, 0)
            for j in range(2):
                normalise(g_chunk[:, j % 2, :], acc[:, j, :], 0).then_inc(g_chunk_ready, 1)
            for b in range(G):
                split_y(4 + b + 1, 0, (USE_PREP[0] + b) % 2, b)
            for j in range(NCH):
                split_x(0, j, j % RING)
                if j + 2 < NCH:
                    normalise(g_chunk[:, j % 2, :], acc[:, j + 2, :], 0).then_inc(g_chunk_ready, 1)
            for k in range(G):
                take_max(0, 0, k, k)

            now = [0]

            def normalise_swap(j):
                dve.wait_ge(g_chunk_loaded[j % 2], 32 * (j // 2 + 1))
                normalise(g_chunk[:, j % 2, :], g_chunk[:, j % 2, :], 1).then_inc(g_chunk_ready, 1)

            def turn(t, parity):
                fixed = isinstance(t, int)
                first, swap, last = fixed and t == 0, fixed and t == SWAP, fixed and t == TG - 1
                units = SWAPPING if swap else PLAIN
                for j in range(NCH):
                    if j == 0 and not (fixed and t >= TG - 1):
                        normalise_group(t + 1, 1 - parity, 0 if now[0] + 1 < GROUPS else 1)
                    if swap:
                        normalise_swap(j)
                    if not first:
                        add_z(t, j)
                    b = j - PREPARE_AT
                    if 0 <= b < G and not (fixed and t >= TG - 1):
                        full = (4 if first else 6) + G * (t + 1) + b + 1
                        if b == 0 and not first:
                            dve.wait_ge(v_rest, 2 * t)
                        split_y(full, 1 - parity, prep_bank(first, b), b)
                    if first and j == PREPARE_AT + G:
                        half_statistics(1, x1_raw, lambda j: dve.wait_ge(x1_loaded, 32))
                        statistics(1)
                    if j == NCH - 1 and not (fixed and t == TG):
                        join_sums(t, parity)
                    for k in range(G * j + G, G * j + 2 * G):
                        if k < UNITS and not (fixed and t == TG):
                            take_max(t, parity, k, units.index(("s", k)) % RING)
                            if k == UNITS - 1:
                                join_maxima(t, parity)
                        if k >= UNITS and not (fixed and t >= TG - 1):
                            take_max(t + 1, 1 - parity, k - UNITS, (k - UNITS) % RING)
                        if swap and k % G == 0:
                            split_x(1, j, units.index(("x", j)) % RING)

            for batch in range(B):
                t0 = batch * GROUPS
                now[0] = t0
                turn(t0, 0)
                start, steps[0] = base[0] + steps[0], 0
                with dve.Fori(t0 + 1, t0 + GROUPS - 1, 2) as t:
                    now[0] = t0 + 1
                    per_turn = G + 6
                    base[0] = (t - (t0 + 1)) * per_turn + start
                    turn(t, 1)
                    turn(t + 1, 0)
                    assert steps[0] == 2 * per_turn
                base[0], steps[0] = start + (GROUPS - 2) * per_turn, 0
                now[0] = t0 + GROUPS - 1
                turn(now[0], 1)
            now[0] = TG
            turn(TG, 0)

        @block.gpsimd
        def _(pool):
            for dst, src in ((theta2_sb, theta2), (W_T_sb, W_T), (biases_sb, biases), (norm_mean_sb, norm_mean),
                             (phi_T2_sb, phi_T2)):
                pool.dma_start(dst[:, :], src).then_inc(weights_loaded, 16)
            pool.wait_ge(zeros_made, 1)
            for h in range(2):
                pool.dma_start(theta_half[h * C:(h + 1) * C, h, :], theta_T2).then_inc(weights_loaded, 16)

            def turn(t, parity):
                if isinstance(t, int) and t == TG:
                    return
                pool.wait_ge(factor_made, t + 1)
                if not (isinstance(t, int) and t == 0):
                    pool.wait_ge(z_made, UNITS * t)
                for j0, j1 in ((1, G), (G, NCH)):
                    nc.gpsimd.tensor_tensor(v_scaled[:, j0:j1, :, :],
                                            v[:, parity, :, :].unsqueeze(1).to_broadcast([P, j1 - j0, G, C]),
                                            factor[:, j0:j1, :].unsqueeze(3).to_broadcast([P, j1 - j0, G, C]),
                                            ALU.mult).then_inc(v_rest, 1)

            turns(pool, turn)


def kernel(x, L0_conv_theta_w, L0_conv_theta_b, L0_conv_phi_w, L0_conv_phi_b, L0_conv_W_w, L0_conv_W_b):
    import numpy as np
    import concourse.bacc as bacc
    from concourse.bass_utils import run_bass_kernel_spmd as run

    x = np.asarray(x)
    B, C, H, W = x.shape
    channel = np.arange(2 * C) % C
    per_group = C // NORM_GROUPS
    same = channel[:, None] // per_group == channel[None, :] // per_group
    arrays = {
        "x": np.ascontiguousarray(x.reshape(B, C, H * W)),
        "theta_T2": np.ascontiguousarray(np.tile(np.asarray(L0_conv_theta_w).T, (1, 2))),
        "theta2": np.ascontiguousarray(np.tile(np.asarray(L0_conv_theta_w), (1, 2))),
        "phi_T2": np.ascontiguousarray(np.tile(np.asarray(L0_conv_phi_w).T, (2, 2))),
        "W_T": np.ascontiguousarray(np.asarray(L0_conv_W_w).T),
        "biases": np.ascontiguousarray(np.stack(
            [np.tile(np.asarray(b), 2) for b in (L0_conv_theta_b, L0_conv_phi_b, L0_conv_W_b)], axis=1)),
        "norm_mean": np.where(same, np.float32(1 / (2 * per_group)), np.float32(0)),
    }
    nc = bacc.Bacc("TRN2", target_bir_lowering=False, num_devices=1)
    args = [nc.dram_tensor(name, a.shape, mybir.dt.from_np(a.dtype), kind="ExternalInput").ap()
            for name, a in arrays.items()]
    out = nc.dram_tensor("out", (B, C, H * W), F32, kind="ExternalOutput").ap()
    attention_kernel(nc, *args, out)
    result = run(nc, [arrays], core_ids=[0])
    return result.results[0]["out"].reshape(B, C, H, W)
```

```python
from contextlib import ExitStack

import concourse.bass as bass
from concourse import mybir


F32 = mybir.dt.float32
F32R = mybir.dt.float32r
I32 = mybir.dt.int32
ACT = mybir.ActivationFunctionType
ALU = mybir.AluOpType
AX = mybir.AxisListType

NORM_GROUPS = 32
NORM_EPS = 1e-5
P = 128
HALF = 512
CHUNK = 2 * HALF
G = 3
RING = 3
PREPARE_AT = 1
LOAD = 3
X_AHEAD = 2
RSQRT_GUESS = 0x5F3759DF
NEWTON_STEPS = 3


def attention_kernel(nc, x, wide_weights, narrow_weights, theta_T2, out):
    B, C, N = x.shape
    NCH = N // CHUNK
    UNITS = NCH * G
    GROUPS = N // (P * G)
    TG = B * GROUPS
    GM = G * P
    SWAP = GROUPS - 1
    assert C * 2 == P and N % CHUNK == 0 and N % GM == 0 and GROUPS % 2 == 0 and B == 2
    assert NCH % LOAD == 0

    with ExitStack() as ctx:
        def sb(name, shape, dt=F32):
            return ctx.enter_context(nc.sbuf_tensor(name, shape, dt))

        def sem(name):
            return ctx.enter_context(nc.semaphore(name))

        probs = sb("probs", [P, UNITS, CHUNK])
        x_parts = sb("x_parts", [P, N], F32R)
        acc = sb("acc", [P, NCH, HALF])
        y_high = sb("y_high", [P, 2, G, P], F32R)
        y_low = sb("y_low", [P, 2, G, P], F32R)
        v = sb("v", [P, 2, G, C])
        v_scaled = sb("v_scaled", [P, NCH, G, C])
        x_group = sb("x_group", [P, 2, GM])
        g_parts = sb("g_parts", [P, 2, GM], F32R)
        g_chunk = sb("g_chunk", [P, 2, HALF])
        x_whole = sb("x_whole", [P, 2, CHUNK])
        wide_weights_sb = sb("wide_weights_sb", [P, 2 * P + 3])
        norm_mean_sb, phi_T2_sb = wide_weights_sb[:, 0:P], wide_weights_sb[:, P:2 * P]
        theta_b, phi_b, W_b = (wide_weights_sb[:, 2 * P + k:2 * P + k + 1] for k in range(3))
        narrow_weights_sb = sb("narrow_weights_sb", [C, P + C])
        theta2_sb, W_T_sb = narrow_weights_sb[:, 0:P], narrow_weights_sb[:, P:P + C]
        theta_half = sb("theta_half", [P, 2, P])
        phi_high = sb("phi_high", [P, P], F32R)
        phi_low = sb("phi_low", [P, P], F32R)
        theta_b_wide = sb("theta_b_wide", [C, P])
        WX_T = sb("WX_T", [P, C])
        WX_parts = sb("WX_parts", [P, 2, C], F32R)
        v_bias = sb("v_bias", [P, C])
        neg_max = sb("neg_max", [P, 2, UNITS])
        neg_max_all = sb("neg_max_all", [P, G])
        max_diff = sb("max_diff", [P, UNITS])
        correction = sb("correction", [P, UNITS])
        chunk_sum = sb("chunk_sum", [P, UNITS])
        corrected_sum = sb("corrected_sum", [P, UNITS - G])
        v_corrected = sb("v_corrected", [P, G, C])
        partial = sb("partial", [P, G])
        total = sb("total", [P, G])
        inv_total = sb("inv_total", [P, G])
        factor = sb("factor", [P, NCH, G])
        bn = sb("bn", [P, NCH, 6])
        half_stat = sb("half_stat", [P, 2])
        mean = sb("mean", [P, B])
        rstd = sb("rstd", [P, B])
        spread = sb("spread", [P, 1])
        second = sb("second", [P, 1])
        variance = sb("variance", [P, 1])
        shifted = sb("shifted", [P, 1], I32)
        guess = sb("guess", [P, 1], I32)
        y0 = sb("y0", [P, 1])
        newton = sb("newton", [P, 1])
        table_load = sb("table_load", [P, 1])

        ring = ctx.enter_context(nc.psum_tensor("ring", [P, RING, CHUNK], F32))
        zbank = ctx.enter_context(nc.psum_tensor("zbank", [P, 2, HALF], F32))

        z_wide = zbank[:, :, :].rearrange("p k n -> p (k n)")

        weights_loaded = sem("weights_loaded")
        x0_loaded = [sem(f"x0_loaded{k}") for k in range(NCH // LOAD)]
        acc_loaded = [sem(f"acc_loaded{j}") for j in range(NCH)]
        x_group_loaded = [sem(f"x_group_loaded{k}") for k in range(2)]
        g_chunk_loaded = [sem(f"g_chunk_loaded{k}") for k in range(2)]
        out_stored = [sem(f"out_stored{k}") for k in range(2)]
        zeros_made = sem("zeros_made")
        wide_made = sem("wide_made")
        weights_split = sem("weights_split")
        half_stat_made = sem("half_stat_made")
        zbank_full = sem("zbank_full")
        zbank_read = sem("zbank_read")
        dve_step = sem("dve_step")
        g_chunk_ready = sem("g_chunk_ready")
        g_group_ready = sem("g_group_ready")
        x_made = sem("x_made")
        x_copied = sem("x_copied")
        x_rounded = sem("x_rounded")
        x_split = sem("x_split")
        bn_taken = sem("bn_taken")
        scores_made = sem("scores_made")
        max_taken = sem("max_taken")
        probs_made = sem("probs_made")
        diff_made = sem("diff_made")
        correction_made = sem("correction_made")
        factor_made = sem("factor_made")
        v_first = sem("v_first")
        v_rest = sem("v_rest")
        z_made = sem("z_made")

        x_halves = x.rearrange("b c (j h n) -> b h c j n", h=2, n=HALF)
        out_halves = out.rearrange("b c (j h n) -> b h c j n", h=2, n=HALF)

        def x_in_slot(rep, j):
            if rep % GROUPS == 0 and rep < TG and j + X_AHEAD < NCH:
                return j + X_AHEAD
            if rep == SWAP and j >= NCH - X_AHEAD:
                return j - (NCH - X_AHEAD)
            return None

        def prepare_slot(rep):
            return NCH - X_AHEAD if rep in (0, SWAP) else PREPARE_AT

        def normalise_slot(rep):
            return STATS_SLOT + 2 if rep == SWAP else 0

        def x_number(rep, j):
            return (rep + 1) // GROUPS * NCH + j

        def x_over_z(rep):
            return rep == 0

        def units_in_order(rep):
            units = [("s", k) for k in range(G)]
            for j in range(NCH):
                if x_in_slot(rep, j) is not None:
                    units.append(("x", x_in_slot(rep, j)))
                units += [("s", k) for k in range(G * j + G, min(G * j + 2 * G, UNITS))]
            return units

        def ring_units(rep):
            return [unit for unit in units_in_order(rep) if unit[0] == "s" or not x_over_z(rep)]

        def ring_start(rep):
            return (X_AHEAD + sum(len(ring_units(r)) for r in range(rep))) % RING

        def ring_place(rep, unit):
            return (ring_start(rep) + ring_units(rep).index(unit)) % RING

        def ring_before(t, rep, unit):
            at = ring_units(rep).index(unit) - RING
            if at >= 0:
                return t, rep, ring_units(rep)[at]
            if rep == 0:
                return (0, 0, ("x", at + X_AHEAD)) if at + X_AHEAD >= 0 else None
            return t - 1, rep - 1, ring_units(rep - 1)[at]

        def z_order(rep):
            order = [("z", j) for j in range(NCH)] if rep else []
            if rep < TG - 1:
                at = prepare_slot(rep) + 1 if rep else 0
                order.insert(at, ("y", 0))
                order.insert(at + 2 if rep else 1, ("v", 0))
            if rep == SWAP:
                order.insert(order.index(("z", STATS_SLOT + 1)), ("mean", 0))
                order.insert(order.index(("z", STATS_SLOT + 2)), ("variance", 0))
            return order

        STATS_SLOT = 4
        EARLY = [("WX", 0), ("v_bias", 0), ("mean", 0), ("variance", 0), ("y", 0), ("v", 0)]
        A_TURN = len(z_order(1))

        def z_use(t, rep, what):
            if rep == 0:
                before = len(EARLY)
            elif rep <= SWAP:
                before = len(EARLY) + len(z_order(0)) + (t - 1) * A_TURN
            else:
                before = len(EARLY) + len(z_order(0)) + (t - 2) * A_TURN + len(z_order(SWAP))
            if rep == TG:
                before += NCH - A_TURN
            return before + z_order(rep).index(what)

        def z_bank(rep, what):
            return z_use(rep, rep, what) % 2

        def z_filled(t, rep, what):
            here = [w for w in z_order(rep) if w[0] != "z"]
            if rep == 0:
                before = len(EARLY)
            elif rep <= SWAP:
                before = len(EARLY) + 2 * t
            else:
                before = len(EARLY) + 2 * t + 2
            return before + here.index(what) + 1

        assert UNITS % RING == 0
        assert z_use(1, 1, ("z", 0)) % 2 == z_use(3, 3, ("z", 0)) % 2
        assert z_use(TG - 2, TG - 2, ("z", 8)) - z_use(SWAP + 1, SWAP + 1, ("z", 8)) == (GROUPS - 2) * A_TURN

        def turns(engine, turn):
            for batch in range(B):
                t0 = batch * GROUPS
                turn(t0, t0)
                with engine.Fori(t0 + 1, t0 + GROUPS - 1, 2) as t:
                    turn(t, t0 + 1)
                    turn(t + 1, t0 + 2)
                turn(t0 + GROUPS - 1, t0 + GROUPS - 1)
            turn(TG, TG)

        block = ctx.enter_context(nc.Block())

        @block.sync
        def _(sp):
            for k in range(NCH // LOAD):
                js = slice(k * LOAD, (k + 1) * LOAD)
                sp.dma_start(acc[0:C, js, :], x_halves[0, 0, :, js, :]).then_inc(x0_loaded[k], 16)

            def load_group(batch, t, parity):
                m0 = (t - batch * GROUPS) * GM
                for h in range(2):
                    sp.dma_start(x_group[h * C:(h + 1) * C, parity, :],
                                 x[batch, :, bass.ds(m0, GM)]).then_inc(x_group_loaded[parity], 16)

            load_group(0, 0, 0)
            load_group(0, 1, 1)

            def load_chunk(n):
                if n < 2:
                    sp.wait_ge(x_made, NCH)
                elif n < NCH + 2:
                    sp.wait_ge(bn_taken, NCH + n - 1)
                else:
                    sp.wait_ge(x_made, n - 1)
                for h in range(2):
                    sp.dma_start(g_chunk[h * C:(h + 1) * C, n % 2, :],
                                 x_halves[1, h, :, n % NCH, :]).then_inc(g_chunk_loaded[n % 2], 16)

            def turn(t, rep, batch):
                if rep + 2 < TG:
                    sp.wait_ge(g_group_ready, t + 1)
                    load_group(batch, t + 2, rep % 2)
                if rep == SWAP:
                    for n in range(NCH + 2):
                        load_chunk(n)
                if rep == GROUPS:
                    load_chunk(NCH + 2)
                if rep in (GROUPS, TG):
                    done = rep // GROUPS - 1
                    for j in range(NCH + 1):
                        if rep == GROUPS and NCH + 3 + j < 2 * NCH:
                            load_chunk(NCH + 3 + j)
                        if j < NCH:
                            sp.wait_ge(zbank_read, z_use(t, rep, ("z", j)) + 1)
                            for h in range(2):
                                sp.dma_start(out_halves[done, h, :, j, :],
                                             acc[h * C:(h + 1) * C, j, :]).then_inc(out_stored[j % 2], 16)
                        if j and rep == GROUPS:
                            sp.wait_ge(out_stored[(j - 1) % 2], 32 * ((j - 1) // 2 + 1))
                            for h in range(2):
                                sp.dma_start(acc[h * C:(h + 1) * C, j - 1, :],
                                             x_halves[1, h, :, j - 1, :]).then_inc(acc_loaded[j - 1], 16)

            for batch in range(B):
                t0 = batch * GROUPS
                turn(t0, t0, batch)
                with sp.Fori(t0 + 1, t0 + GROUPS - 3, 2) as t:
                    turn(t, t0 + 1, batch)
                    turn(t + 1, t0 + 2, batch)
                for t in range(t0 + GROUPS - 3, t0 + GROUPS):
                    turn(t, t, (t + 2) // GROUPS)
            turn(TG, TG, None)
            for k in range(2):
                sp.wait_ge(out_stored[k], 32 * B * len(range(k, NCH, 2)))

        @block.tensor
        def _(pe):
            made = [None]

            def use_z_bank(use):
                if not isinstance(use, int) or use >= 2:
                    pe.wait_ge(zbank_read, use - 1)
                if made[0] is not None:
                    pe.wait_ge(x_copied, made[0])
                    made[0] = None

            def use_ring(t, rep, unit):
                before = ring_before(t, rep, unit)
                if before:
                    t, rep, (kind, k) = before
                    if kind == "s":
                        pe.wait_ge(probs_made, UNITS * t + k + 1)
                    else:
                        pe.wait_ge(x_copied, x_number(rep, k) + 1)

            def x_chunk(number, to):
                pe.wait_ge(g_chunk_ready, number + 1)
                for h in range(2):
                    last = nc.tensor.matmul(to[:, h * HALF:(h + 1) * HALF], theta_half[:, h, :],
                                            g_chunk[:, number % 2, :], start=True, stop=True)
                last.then_inc(x_made, 1)

            def scores(t, rep, k):
                j, b = k // G, k % G
                use_ring(t, rep, ("s", k))
                if k == 0:
                    if rep == 0:
                        pe.wait_ge(zbank_read, EARLY.index(("y", 0)) + 1)
                    else:
                        pe.wait_ge(zbank_read, z_use(t - 1, rep - 1, ("y", 0)) + 1)
                if rep % GROUPS == 0 and b == 0:
                    pe.wait_ge(x_split, x_number(rep, j) + 1)
                place = ring_place(rep, ("s", k))
                for part in (y_high, y_low):
                    for h in range(2):
                        n0 = j * CHUNK + h * HALF
                        last = nc.tensor.matmul(ring[:, place, h * HALF:(h + 1) * HALF],
                                                part[:, rep % 2, b, :], x_parts[:, n0:n0 + HALF],
                                                start=(part is y_high), stop=(part is y_low))
                last.then_inc(scores_made, 1)

            def second_product(t, rep, j):
                if j == 0:
                    pe.wait_ge(v_first, t)
                if j == 1:
                    pe.wait_ge(v_rest, 2 * t - 1)
                if j == G:
                    pe.wait_ge(v_rest, 2 * t)
                use_z_bank(z_use(t, rep, ("z", j)))
                for b in range(G):
                    for h in range(2):
                        last = nc.tensor.matmul(zbank[h * C:(h + 1) * C, z_bank(rep, ("z", j)), :],
                                                v_scaled[:, j, b, :],
                                                probs[:, G * j + b, h * HALF:(h + 1) * HALF],
                                                start=(b == 0), stop=(b == G - 1))
                    last.then_inc(z_made, 1)

            def make_y(use, bank, parity, ready):
                pe.wait_ge(g_group_ready, ready)
                use_z_bank(use)
                for part in (phi_high, phi_low):
                    last = nc.tensor.matmul(zbank[:, bank, 0:GM], part[:, :], g_parts[:, parity, :],
                                            start=(part is phi_high), stop=(part is phi_low))
                last.then_inc(zbank_full, 1)

            def make_v(use, bank, parity):
                use_z_bank(use)
                for b in range(G):
                    last = nc.tensor.matmul(zbank[:, bank, b * 2 * C:(b + 1) * 2 * C],
                                            g_parts[:, parity, b * P:(b + 1) * P],
                                            WX_parts[:, :, :].rearrange("p h c -> p (h c)"),
                                            start=True, stop=True)
                last.then_inc(zbank_full, 1)

            def mean_over_group(use, bank, ready, stat):
                pe.wait_ge(half_stat_made, ready)
                use_z_bank(use)
                nc.tensor.matmul(zbank[:, bank, 0:1], norm_mean_sb, stat, start=True, stop=True
                                 ).then_inc(zbank_full, 1)

            pe.wait_ge(weights_loaded, 16 * 4)
            nc.tensor.matmul(zbank[:, 0, 0:C], theta2_sb, W_T_sb, start=True, stop=True
                             ).then_inc(zbank_full, 1)
            pe.wait_ge(wide_made, 1)
            nc.tensor.matmul(zbank[:, 1, 0:C], theta_b_wide[:, :], W_T_sb, start=True, stop=True
                             ).then_inc(zbank_full, 1)
            mean_over_group(2, 0, 1, half_stat[:, 0:1])
            mean_over_group(3, 1, 2, second[:, 0:1])
            x_chunk(0, ring[:, 0, :])
            pe.wait_ge(weights_split, 2)
            make_y(4, 0, 0, 1)
            make_v(5, 1, 0)
            x_chunk(1, ring[:, 1, :])
            for k in range(G):
                scores(0, 0, k)

            def turn(t, rep):
                for j in range(NCH):
                    if rep:
                        second_product(t, rep, j)
                    if j == prepare_slot(rep) and rep < TG - 1:
                        make_y(z_use(t, rep, ("y", 0)), z_bank(rep, ("y", 0)), 1 - rep % 2, t + 2)
                    if j == prepare_slot(rep) + 1 and rep < TG - 1:
                        make_v(z_use(t, rep, ("v", 0)), z_bank(rep, ("v", 0)), 1 - rep % 2)
                    if rep == SWAP and j == STATS_SLOT:
                        mean_over_group(z_use(t, rep, ("mean", 0)), z_bank(rep, ("mean", 0)), 3, half_stat[:, 0:1])
                    if rep == SWAP and j == STATS_SLOT + 1:
                        mean_over_group(z_use(t, rep, ("variance", 0)), z_bank(rep, ("variance", 0)), 4,
                                        second[:, 0:1])
                    x = x_in_slot(rep, j)
                    if x is not None:
                        if x_over_z(rep):
                            pe.wait_ge(zbank_read, len(EARLY))
                            pe.wait_ge(x_copied, x_number(rep, x))
                            x_chunk(x_number(rep, x), z_wide)
                            made[0] = x_number(rep, x) + 1
                        else:
                            use_ring(t, rep, ("x", x))
                            x_chunk(x_number(rep, x), ring[:, ring_place(rep, ("x", x)), :])
                    for k in range(G * j + G, G * j + 2 * G):
                        if k < UNITS and rep < TG:
                            scores(t, rep, k)
                        if k >= UNITS and rep < TG - 1:
                            scores(t + 1, rep + 1, k - UNITS)

            turns(pe, turn)

        @block.scalar
        def _(act):
            def copy_x(number, source):
                act.wait_ge(x_made, number + 1)
                if number >= 2:
                    act.wait_ge(x_split, number - 1)
                nc.scalar.activation(x_whole[:, number % 2, :], source, ACT.Identity,
                                     bias=theta_b).then_inc(x_copied, 1)

            for k in range(NCH // LOAD):
                js = slice(k * LOAD, (k + 1) * LOAD)
                act.dma_start(acc[C:P, js, :], x_halves[0, 1, :, js, :]).then_inc(x0_loaded[k], 16)
            act.wait_ge(zeros_made, 1)
            nc.scalar.activation(table_load[:, :], table_load[:, :], ACT.Exp)
            act.wait_ge(weights_loaded, 16 * 4)
            for j in range(X_AHEAD):
                copy_x(j, ring[:, j, :])

            def turn(t, rep):
                if rep == TG:
                    return
                order = units_in_order(rep)
                for i in range(1, len(order)):
                    if order[i][0] == "x" and x_over_z(rep):
                        order[i - 1], order[i] = order[i], order[i - 1]
                for kind, k in order:
                    if kind == "x":
                        copy_x(x_number(rep, k), z_wide if x_over_z(rep) else ring[:, ring_place(rep, ("x", k)), :])
                        continue
                    place = ring_place(rep, ("s", k))
                    if k == UNITS - 1:
                        act.wait_ge(diff_made, t + 1)
                        nc.scalar.activation(correction[:, :], max_diff[:, :], ACT.Exp
                                             ).then_inc(correction_made, 1)
                    act.wait_ge(max_taken, UNITS * t + k + 1)
                    if rep:
                        act.wait_ge(z_made, UNITS * (t - 1) + k + 1)
                    nc.scalar.activation(probs[:, k, :], ring[:, place, :], ACT.Exp,
                                         bias=neg_max[:, rep % 2, k:k + 1],
                                         accum_out=chunk_sum[:, k:k + 1]).then_inc(probs_made, 1)

            turns(act, turn)

        @block.vector
        def _(dve):
            steps = [0]
            base = [0]

            def link(ins):
                steps[0] += 1
                ins.then_inc(dve_step, 1)
                dve.wait_ge(dve_step, base[0] + steps[0])

            def mean_of_halves(batch):
                dve.wait_ge(bn_taken, NCH * (batch + 1))
                nc.vector.bn_aggr(half_stat[:, :], bn[:, :, :].rearrange("p j s -> p (j s)")
                                  ).then_inc(half_stat_made, 1)

            def second_moment(batch, bank, full, use):
                dve.wait_ge(zbank_full, full)
                nc.vector.tensor_copy(mean[:, batch:batch + 1], zbank[:, bank, 0:1]).then_inc(zbank_read, 1)
                dve.wait_ge(zbank_read, use + 1)
                dve.wait_ge(half_stat_made, 2 * batch + 1)
                link(nc.vector.tensor_tensor(spread[:, :], half_stat[:, 0:1], mean[:, batch:batch + 1], ALU.subtract))
                nc.vector.scalar_tensor_tensor(second[:, :], spread[:, :], spread[:, :], half_stat[:, 1:2],
                                               ALU.mult, ALU.add).then_inc(half_stat_made, 1)

            def inverse_root(batch, bank, full, use):
                dve.wait_ge(zbank_full, full)
                nc.vector.tensor_scalar(variance[:, :], zbank[:, bank, 0:1], NORM_EPS, None,
                                        ALU.add).then_inc(zbank_read, 1)
                dve.wait_ge(zbank_read, use + 1)
                link(nc.vector.tensor_scalar(shifted[:, :], variance[:, :].bitcast(I32), 1, None,
                                             ALU.logical_shift_right))
                link(nc.vector.tensor_scalar(guess[:, :], shifted[:, :], -1.0, float(RSQRT_GUESS),
                                             ALU.mult, ALU.add))
                root = guess[:, :].bitcast(F32)
                for s in range(NEWTON_STEPS):
                    link(nc.vector.scalar_tensor_tensor(y0[:, :], root, variance[:, :], root, ALU.mult, ALU.mult))
                    link(nc.vector.tensor_scalar(newton[:, :], y0[:, :], -0.5, 1.5, ALU.mult, ALU.add))
                    to = rstd[:, batch:batch + 1] if s == NEWTON_STEPS - 1 else second[:, :]
                    link(nc.vector.tensor_tensor(to, root, newton[:, :], ALU.mult))
                    root = to

            def normalise(dst, src, batch, p0=0, p1=P):
                return nc.vector.tensor_scalar(dst, src, mean[p0:p1, batch:batch + 1], rstd[p0:p1, batch:batch + 1],
                                               ALU.subtract, ALU.mult)

            def normalise_chunk(number):
                batch, j = number // NCH, number % NCH
                g = g_chunk[:, number % 2, :]
                if batch == 0:
                    if number >= 2:
                        dve.wait_ge(x_made, number - 1)
                    src = acc[:, j, :]
                else:
                    dve.wait_ge(g_chunk_loaded[number % 2], 32 * (number // 2 + 1))
                    src = g
                normalise(g, src, batch).then_inc(g_chunk_ready, 1)

            def normalise_group(t, rep):
                batch, parity = rep // GROUPS, rep % 2
                dve.wait_ge(x_group_loaded[parity], 16 * (t + 2 - parity))
                link(normalise(g_parts[:, parity, :], x_group[:, parity, :], batch))
                lower = x_group[C:P, parity, :]
                link(normalise(lower, lower, batch, C, P))
                low = g_parts[C:P, parity, :]
                nc.vector.tensor_tensor(low, lower, low.bitcast(F32), ALU.subtract).then_inc(g_group_ready, 1)

            def round_x(number):
                batch, j = number // NCH, number % NCH
                dve.wait_ge(x_copied, number + 1)
                if batch:
                    dve.wait_ge(scores_made, UNITS * SWAP + G * j + G)
                nc.vector.tensor_copy(x_parts[:, j * CHUNK:(j + 1) * CHUNK], x_whole[:, number % 2, :]
                                      ).then_inc(x_rounded, 1)

            def split_y(full, parity, bank):
                dve.wait_ge(zbank_full, full)
                high = y_high[:, parity, :, :].rearrange("p b m -> p (b m)")
                low = y_low[:, parity, :, :].rearrange("p b m -> p (b m)")
                link(nc.vector.tensor_scalar(high, zbank[:, bank, 0:GM], phi_b, None, ALU.add))
                nc.vector.scalar_tensor_tensor(low, zbank[:, bank, 0:GM], phi_b, high.bitcast(F32),
                                               ALU.add, ALU.subtract).then_inc(zbank_read, 1)

            def take_v(full, parity, bank):
                dve.wait_ge(zbank_full, full)
                by_part = zbank[:, bank, 0:G * 2 * C].rearrange("p (b h c) -> p h b c", b=G, h=2)
                link(nc.vector.tensor_tensor(v[:, parity, :, :], by_part[:, 0],
                                             v_bias[:, :].unsqueeze(1).to_broadcast([P, G, C]), ALU.add))
                nc.vector.tensor_tensor(v[:, parity, :, :], by_part[:, 1], v[:, parity, :, :],
                                        ALU.add).then_inc(zbank_read, 1)

            def add_z(t, rep, j):
                dve.wait_ge(z_made, UNITS * (t - 1) + G * j + G)
                if rep > GROUPS:
                    dve.wait_ge(acc_loaded[j], 32)
                src = zbank[:, z_bank(rep, ("z", j)), :]
                if rep % GROUPS == 0:
                    ins = nc.vector.scalar_tensor_tensor(acc[:, j, :], src, W_b, acc[:, j, :], ALU.add, ALU.add)
                else:
                    ins = nc.vector.tensor_tensor(acc[:, j, :], src, acc[:, j, :], ALU.add)
                ins.then_inc(zbank_read, 1)

            def take_max(t, rep, k):
                dve.wait_ge(scores_made, UNITS * t + k + 1)
                nc.vector.tensor_reduce(neg_max[:, rep % 2, k:k + 1], ring[:, ring_place(rep, ("s", k)), :],
                                        AX.X, ALU.max, negate=True).then_inc(max_taken, 1)

            def join_maxima(t, parity):
                dve.wait_ge(max_taken, UNITS * t + UNITS)
                chunk_max = neg_max[:, parity, :].rearrange("p (j b) -> p j b", b=G)
                link(nc.vector.tensor_reduce(neg_max_all[:, :], chunk_max.rearrange("p j b -> p b j"), AX.X, ALU.min))
                nc.vector.tensor_tensor(max_diff[:, :].rearrange("p (j b) -> p j b", b=G),
                                        neg_max_all[:, :].unsqueeze(1).to_broadcast([P, NCH, G]),
                                        chunk_max, ALU.subtract).then_inc(diff_made, 1)

            def sum_chunks(t, parity):
                dve.wait_ge(correction_made, t + 1)
                early = UNITS - G
                link(nc.vector.tensor_tensor(corrected_sum[:, :], chunk_sum[:, 0:early], correction[:, 0:early],
                                             ALU.mult))
                link(nc.vector.tensor_reduce(partial[:, :], corrected_sum[:, :].rearrange("p (j b) -> p b j", b=G),
                                             AX.X, ALU.add))
                link(nc.vector.tensor_tensor(v_corrected[:, :, :], v[:, parity, :, :],
                                             correction[:, 0:G].unsqueeze(2).to_broadcast([P, G, C]), ALU.mult))

            def join_sums(t, parity):
                for b in range(G):
                    k = UNITS - G + b
                    dve.wait_ge(probs_made, UNITS * t + k + 1)
                    ins = nc.vector.scalar_tensor_tensor(total[:, b:b + 1], chunk_sum[:, k:k + 1],
                                                         correction[:, k:k + 1], partial[:, b:b + 1],
                                                         ALU.mult, ALU.add)
                    ins.then_inc(dve_step, 1)
                    steps[0] += 1
                dve.wait_ge(dve_step, base[0] + steps[0])
                link(nc.vector.reciprocal(inv_total[:, :], total[:, :]))
                nc.vector.tensor_tensor(v_scaled[:, 0, :, :], v_corrected[:, :, :],
                                        inv_total[:, :].unsqueeze(2).to_broadcast([P, G, C]),
                                        ALU.mult).then_inc(v_first, 1)
                nc.vector.tensor_tensor(factor[:, :, :], correction[:, :].rearrange("p (j b) -> p j b", b=G),
                                        inv_total[:, :].unsqueeze(1).to_broadcast([P, NCH, G]),
                                        ALU.mult).then_inc(factor_made, 1)

            nc.vector.memset(table_load[:, :], 0.0)
            nc.vector.memset(theta_half[:, :, :], 0.0).then_inc(zeros_made, 1)

            def take_x0(pieces):
                for k in pieces:
                    dve.wait_ge(x0_loaded[k], 32)
                    for j in range(k * LOAD, (k + 1) * LOAD):
                        nc.vector.bn_stats(bn[:, j, :], acc[:, j, :]).then_inc(bn_taken, 1)

            take_x0([0, 1])
            dve.wait_ge(weights_loaded, 16 * 4)
            nc.vector.tensor_copy(theta_b_wide[:, :], theta_b[0:C].to_broadcast([C, P])).then_inc(wide_made, 1)
            dve.wait_ge(zbank_full, 1)
            nc.vector.tensor_copy(WX_T[:, :], zbank[:, 0, 0:C]).then_inc(zbank_read, 1)
            dve.wait_ge(zbank_full, 2)
            nc.vector.tensor_copy(v_bias[:, :], zbank[:, 1, 0:C]).then_inc(zbank_read, 1)
            dve.wait_ge(zbank_read, 1)
            for whole, high, low in ((WX_T[:, :], WX_parts[:, 0, :], WX_parts[:, 1, :]),
                                     (phi_T2_sb, phi_high[:, :], phi_low[:, :])):
                link(nc.vector.tensor_copy(high, whole))
                nc.vector.tensor_tensor(low, whole, high.bitcast(F32), ALU.subtract).then_inc(weights_split, 1)
            take_x0([2])
            mean_of_halves(0)
            second_moment(0, 0, 3, 2)
            inverse_root(0, 1, 4, 3)
            for number in range(X_AHEAD):
                normalise_chunk(number)
            normalise_group(0, 0)
            round_x(0)
            normalise_chunk(X_AHEAD)
            split_y(5, 0, 0)
            take_v(6, 0, 1)
            round_x(1)
            for k in range(G):
                take_max(0, 0, k)

            def turn(t, rep):
                parity = rep % 2
                for j in range(NCH):
                    if j == normalise_slot(rep) and rep < TG - 1:
                        normalise_group(t + 1, rep + 1)
                    if rep == SWAP:
                        for n in range(2 * j, min(2 * j + 2, NCH)):
                            dve.wait_ge(g_chunk_loaded[n % 2], 32 * (n // 2 + 1))
                            nc.vector.bn_stats(bn[:, n, :], g_chunk[:, n % 2, :]).then_inc(bn_taken, 1)
                        if j == STATS_SLOT:
                            mean_of_halves(1)
                    x = x_in_slot(rep, j)
                    at, i = (rep, j + 1) if j < NCH - 1 else (rep + 1, 0)
                    following = None if x_in_slot(at, i) is None else x_number(at, x_in_slot(at, i))
                    if rep:
                        add_z(t, rep, j)
                    if j == NCH - 1 and rep < TG:
                        sum_chunks(t, parity)
                    if j == prepare_slot(rep) and rep < TG - 1:
                        split_y(z_filled(t, rep, ("y", 0)), 1 - parity, z_bank(rep, ("y", 0)))
                    if j == prepare_slot(rep) + 1 and rep < TG - 1:
                        if rep:
                            dve.wait_ge(v_rest, 2 * t)
                        take_v(z_filled(t, rep, ("v", 0)), 1 - parity, z_bank(rep, ("v", 0)))
                    if j == NCH - 1 and rep < TG:
                        join_sums(t, parity)
                    if following is not None:
                        normalise_chunk(following)
                    if x is not None and x_over_z(rep):
                        round_x(x_number(rep, x))
                    for k in range(G * j + G, G * j + 2 * G):
                        if k < UNITS and rep < TG:
                            take_max(t, rep, k)
                            if k == UNITS - 1:
                                join_maxima(t, parity)
                        if k >= UNITS and rep < TG - 1:
                            take_max(t + 1, rep + 1, k - UNITS)
                        if x is not None and k % G == 0 and not x_over_z(rep):
                            round_x(x_number(rep, x))
                    if rep == SWAP and j == STATS_SLOT:
                        second_moment(1, z_bank(rep, ("mean", 0)), z_filled(t, rep, ("mean", 0)),
                                      z_use(t, rep, ("mean", 0)))
                    if rep == SWAP and j == STATS_SLOT + 1:
                        inverse_root(1, z_bank(rep, ("variance", 0)), z_filled(t, rep, ("variance", 0)),
                                     z_use(t, rep, ("variance", 0)))

            per_turn = 12
            for batch in range(B):
                t0 = batch * GROUPS
                turn(t0, t0)
                start, steps[0] = base[0] + steps[0], 0
                with dve.Fori(t0 + 1, t0 + GROUPS - 1, 2) as t:
                    base[0] = (t - (t0 + 1)) * per_turn + start
                    turn(t, t0 + 1)
                    turn(t + 1, t0 + 2)
                    assert steps[0] == 2 * per_turn
                base[0], steps[0] = start + (GROUPS - 2) * per_turn, 0
                turn(t0 + GROUPS - 1, t0 + GROUPS - 1)
            turn(TG, TG)

        @block.gpsimd
        def _(pool):
            for dst, src in ((narrow_weights_sb, narrow_weights), (wide_weights_sb, wide_weights)):
                pool.dma_start(dst[:, :], src).then_inc(weights_loaded, 16)
            pool.wait_ge(zeros_made, 1)
            for h in range(2):
                pool.dma_start(theta_half[h * C:(h + 1) * C, h, :], theta_T2).then_inc(weights_loaded, 16)

            def split_x(number, scaled):
                if scaled:
                    pool.wait_ge(v_rest, scaled)
                pool.wait_ge(x_rounded, number + 1)
                j = number % NCH
                low = x_parts[C:P, j * CHUNK:(j + 1) * CHUNK]
                nc.gpsimd.tensor_tensor(low, x_whole[C:P, number % 2, :], low.bitcast(F32),
                                        ALU.subtract).then_inc(x_split, 1)

            for number in range(X_AHEAD):
                split_x(number, 0)

            def turn(t, rep):
                if rep == TG:
                    return
                for j in range(NCH):
                    if j == NCH - 1:
                        pool.wait_ge(factor_made, t + 1)
                        if x_in_slot(rep, j - 1) is not None or rep % GROUPS == 0:
                            pool.wait_ge(x_split, x_number(rep, NCH - 1 if rep % GROUPS == 0 else 0) + 1)
                        if rep:
                            pool.wait_ge(z_made, UNITS * t)
                        for j0, j1 in ((1, G), (G, NCH)):
                            nc.gpsimd.tensor_tensor(
                                v_scaled[:, j0:j1, :, :],
                                v[:, rep % 2, :, :].unsqueeze(1).to_broadcast([P, j1 - j0, G, C]),
                                factor[:, j0:j1, :].unsqueeze(3).to_broadcast([P, j1 - j0, G, C]),
                                ALU.mult).then_inc(v_rest, 1)
                    x = x_in_slot(rep, j)
                    if x is not None:
                        split_x(x_number(rep, x), 2 * t + (2 if j == NCH - 1 else 0))

            turns(pool, turn)


def kernel(x, L0_conv_theta_w, L0_conv_theta_b, L0_conv_phi_w, L0_conv_phi_b, L0_conv_W_w, L0_conv_W_b):
    import numpy as np
    import concourse.bacc as bacc
    from concourse.bass_utils import run_bass_kernel_spmd as run

    x = np.asarray(x)
    B, C, H, W = x.shape
    channel = np.arange(2 * C) % C
    per_group = C // NORM_GROUPS
    same = channel[:, None] // per_group == channel[None, :] // per_group
    theta, phi, W_out, theta_b, phi_b, W_b = (np.asarray(a) for a in (
        L0_conv_theta_w, L0_conv_phi_w, L0_conv_W_w, L0_conv_theta_b, L0_conv_phi_b, L0_conv_W_b))
    norm_mean = np.where(same, np.float32(1 / (2 * per_group)), np.float32(0))
    biases = np.stack([np.tile(b, 2) for b in (theta_b, phi_b, W_b)], axis=1)
    arrays = {
        "x": np.ascontiguousarray(x.reshape(B, C, H * W)),
        "wide_weights": np.concatenate([norm_mean, np.tile(phi.T, (2, 2)), biases], axis=1),
        "narrow_weights": np.concatenate([np.tile(theta, (1, 2)), W_out.T], axis=1),
        "theta_T2": np.ascontiguousarray(np.tile(theta.T, (1, 2))),
    }
    nc = bacc.Bacc("TRN2", target_bir_lowering=False, num_devices=1)
    args = [nc.dram_tensor(name, a.shape, mybir.dt.from_np(a.dtype), kind="ExternalInput").ap()
            for name, a in arrays.items()]
    out = nc.dram_tensor("out", (B, C, H * W), F32, kind="ExternalOutput").ap()
    attention_kernel(nc, *args, out)
    result = run(nc, [arrays], core_ids=[0])
    return result.results[0]["out"].reshape(B, C, H, W)
```
